# Optimizing a Trainium2 kernel written in Bass

```python
import numpy as np
import jax
import jax.numpy as jnp

def _softmax(x, axis=-1):
    return jax.nn.softmax(x, axis=axis)

def _gelu(x):
    return jax.nn.gelu(x, approximate=True)

def _silu(x):
    return jax.nn.silu(x)

def _sigmoid(x):
    return jax.nn.sigmoid(x)

def _layernorm(x, axis=-1, eps=1e-05):
    m = jnp.mean(x, axis=axis, keepdims=True)
    v = jnp.var(x, axis=axis, keepdims=True)
    return (x - m) / jnp.sqrt(v + eps)

def _scatter_add(tgt, idx, src, axis=0):
    return tgt.at[idx].add(src)

def _segment_sum(src, seg, n):
    return jax.ops.segment_sum(src, seg, n)
kernel_name = 'mk_adj_preln_d1_adj_r2_1bc152'

def setup_inputs(seed: int=0):
    np.random.seed(seed)
    _w = jnp.asarray

    def _rec_inputs():
        import jax
        import jax.numpy as jnp
        _gk = jax.random.key(seed)
        x = -0.0002928 + 1 * jax.random.normal(jax.random.fold_in(_gk, 1), (4096, 256), jnp.float32)
        _w = (1.0 + jnp.arange(4096, dtype=jnp.float32)) ** (-0.5)
        _w = _w / _w.mean()
        _pij = jnp.clip(0.00195312 * _w[:, None] * _w[None, :], 0.0, 1.0)
        _a = jax.random.uniform(jax.random.fold_in(_gk, 2), (4096, 4096)) < _pij
        _a = jnp.logical_or(_a, jnp.swapaxes(_a, -1, -2))
        _a = jnp.logical_or(_a, jnp.eye(4096, dtype=bool))
        _af = _a.astype(jnp.float32)
        _af = _af * jax.random.uniform(jax.random.fold_in(_gk, 3), (4096, 4096), jnp.float32, 0.05, 5.41998)
        adj = _af
        return (x, adj)
    x, adj = _rec_inputs()

    def _L0_gnn_setup():
        import jax, jax.numpy as jnp
        import numpy as np
        N = 4096
        D = 256
        key = jax.random.key(seed)
        ks = jax.random.split(key, 6)
        s = 1.0 / np.sqrt(D)
        return {'x': jax.random.normal(ks[0], (N, D), jnp.float32), 'spatial_encoding': jax.random.normal(ks[1], (N, N), jnp.float32), 'edge_encoding': jax.random.normal(ks[2], (N, N), jnp.float32), 'Wq': jax.random.normal(ks[3], (D, D), jnp.float32) * s, 'bq': jnp.zeros((D,), jnp.float32), 'Wk': jax.random.normal(ks[4], (D, D), jnp.float32) * s, 'bk': jnp.zeros((D,), jnp.float32), 'Wv': jax.random.normal(ks[5], (D, D), jnp.float32) * s, 'bv': jnp.zeros((D,), jnp.float32)}
    _L0_gnn_all = _L0_gnn_setup()
    _L0_gnn_in = {k: v for k, v in _L0_gnn_all.items() if k in ('Wq', 'bq', 'Wk', 'bk', 'Wv', 'bv')}
    del _L0_gnn_all
    return {'x': x, 'adj': adj, 'L0_gnn_Wq': _L0_gnn_in['Wq'], 'L0_gnn_bq': _L0_gnn_in['bq'], 'L0_gnn_Wk': _L0_gnn_in['Wk'], 'L0_gnn_bk': _L0_gnn_in['bk'], 'L0_gnn_Wv': _L0_gnn_in['Wv'], 'L0_gnn_bv': _L0_gnn_in['bv']}

def reference(x, adj, L0_gnn_Wq, L0_gnn_bq, L0_gnn_Wk, L0_gnn_bk, L0_gnn_Wv, L0_gnn_bv):
    import jax
    import jax.numpy as jnp

    def _L0_gnn_ref(x, spatial_encoding, edge_encoding, Wq, bq, Wk, bk, Wv, bv):
        import jax, jax.numpy as jnp
        import numpy as np
        N = 4096
        D = 256
        q = x @ Wq.T + bq
        k = x @ Wk.T + bk
        v = x @ Wv.T + bv
        scale = 1.0 / jnp.sqrt(jnp.asarray(q.shape[-1], q.dtype))
        a = q @ k.T * scale + spatial_encoding + edge_encoding
        attn = jax.nn.softmax(a, axis=-1)
        return attn @ v
    h = jnp.maximum(_layernorm(x, axis=-1), 0.0)
    x = x + _L0_gnn_ref(h, adj, adj, L0_gnn_Wq, L0_gnn_bq, L0_gnn_Wk, L0_gnn_bk, L0_gnn_Wv, L0_gnn_bv)
    return x

_drawn_inputs = setup_inputs


def setup_inputs(seed=0):
    import zlib

    import numpy as np

    out = dict(_drawn_inputs(seed))
    spreads = {'L0_gnn_bq': (0.0, 0.71), 'L0_gnn_bk': (0.0, 0.8), 'L0_gnn_bv': (0.0, 0.1)}
    factors = {}
    for name, (base, spread) in spreads.items():
        noise = np.random.default_rng([zlib.crc32(name.encode()), seed]).standard_normal(out[name].shape)
        drawn = base * np.exp(spread * noise) if base else spread * noise
        out[name] = jnp.asarray(drawn.astype(out[name].dtype))
    for name, factor in factors.items():
        out[name] = (out[name] * factor).astype(out[name].dtype)
    return out
```

```python
import concourse.bass as bass
from concourse import mybir
from contextlib import ExitStack


def graph_attention_kernel(nc, x, adj, wq, bq, wk, bk, wv, bv, out):
    f32 = mybir.dt.float32
    f32r = mybir.dt.float32r
    ALU = mybir.AluOpType
    ACT = mybir.ActivationFunctionType
    AX = mybir.AxisListType

    P = 128
    N, D = x.shape
    DB = D // P
    BANK = 512
    TILES = N // P
    CH = N // BANK
    KB = BANK // P
    GROUPS = N // BANK
    GT = BANK // P
    SB = 4
    QT = 4
    QC = CH // QT
    EPS = 1e-5
    QSCALE = 0.5 * float(D) ** -0.5
    LOWEST = -3.4028234663852886e38

    x_groups = x.rearrange("(g j p) d -> g p j d", p=P, j=GT)
    x_tiles = x.rearrange("(t p) d -> t p d", p=P)
    out_tiles = out.rearrange("(t p) d -> t p d", p=P)
    adj_tiles = adj.rearrange("(t p) n -> t p n", p=P)

    ctx = ExitStack()
    with ctx:
        def sb(name, shape, dt=f32):
            return ctx.enter_context(nc.sbuf_tensor(name, shape, dt))

        def sem(name):
            return ctx.enter_context(nc.semaphore(name))

        q_spill = nc.dram_tensor("q_spill", [GROUPS, GT, P, DB, P], f32, kind="Internal").ap()

        kT = sb("kT", [P, 2, DB, N], f32r)
        v = sb("v", [P, TILES, 2, D], f32r)
        logits = sb("logits", [P, 2, N])
        pT = sb("pT", [P, 2, 2, BANK], f32r)
        wT = sb("wT", [P, 3, 2, DB, D], f32r)
        hT = sb("hT", [P, 2, 2, DB, BANK], f32r)
        qhl = sb("qhl", [P, 2, 2, DB, P], f32r)
        ident = sb("ident", [P, P])
        row_io = sb("row_io", [P, 2, 2, D])
        half_out = sb("half_out", [P, 2, D])
        x_res = row_io[:, 0, :, :]
        q_raw = row_io[:, 1, :, :].rearrange("p b (k q) -> p b k q", k=DB)
        v_sum = row_io[:, :, :, :]
        bv_rows = half_out[:, :, :]
        w_nat = logits[:, 0, 0:3 * DB * D].rearrange("p (w o i) -> p w o i", w=3, o=DB)
        x_rows = logits[:, 1, 0:2 * GT * D].rearrange("p (b j d) -> p b j d", b=2, j=GT)
        q_out = logits[:, 1, 2 * GT * D:2 * GT * D + 2 * DB * BANK]\
            .rearrange("p (b k r) -> p b k r", b=2, k=DB)

        bq_col = sb("bq_col", [P, DB])
        bqs_col = sb("bqs_col", [P, DB])
        bk_col = sb("bk_col", [P, DB])
        stats = sb("stats", [P, GT, 6])
        mean_var = sb("mean_var", [P, 2, GT, 2])
        var_eps = sb("var_eps", [P, 2, GT])
        minus_half = sb("minus_half", [P, GT])
        rstd = sb("rstd", [P, 2, GT])
        chunk_max = sb("chunk_max", [P, 2, CH])
        neg_max = sb("neg_max", [P, 2])
        chunk_sum = sb("chunk_sum", [P, 2, CH])
        row_sum = sb("row_sum", [P, 1])
        inv_sum = sb("inv_sum", [P, 1])
        zero_col = sb("zero_col", [P, 1])

        ps = ctx.enter_context(nc.psum_tensor("ps", [P, 8, BANK], f32))
        PT_BANK, O_BANK = 4, 6

        s_passed = sem("waits_passed")
        s_w = sem("w_loaded")
        s_bias = sem("bias_loaded")
        s_x = [sem(f"x_rows_loaded{b}") for b in range(2)]
        s_adj = [[sem(f"adj_loaded{b}_{n}") for n in range(QT)] for b in range(2)]
        s_xr = [sem(f"x_res_loaded{b}") for b in range(2)]
        s_qin = [sem(f"q_loaded{b}") for b in range(2)]
        s_qst = [sem(f"q_spilled{b}") for b in range(2)]
        s_out = [sem(f"out_stored{b}") for b in range(2)]
        s_zero = sem("ident_zeroed")
        s_ident = sem("ident_made")
        s_const = sem("constants_made")
        s_wt = sem("w_transposed")
        s_whi = sem("w_hi_written")
        s_wlo = sem("w_lo_written")
        s_bqs = sem("bq_scaled")
        s_stat = sem("bn_stats_done")
        s_mv = sem("mean_var_ready")
        s_ve = sem("var_eps_ready")
        s_rstd = sem("rstd_ready")
        s_norm = sem("h_normalized")
        s_ht = sem("h_transposed")
        s_hhi = sem("h_hi_written")
        s_hlo = sem("h_lo_written")
        s_kmm = sem("k_projected")
        s_qmm = sem("q_projected")
        s_vmm = sem("v_projected")
        s_khi = sem("k_hi_written")
        s_klo = sem("k_lo_written")
        s_qw = sem("q_written")
        s_vs = sem("v_biased")
        s_vhi = sem("v_hi_written")
        s_vlo = sem("v_lo_written")
        s_qhi = sem("q_hi_written")
        s_qlo = sem("q_lo_written")
        s_score = sem("scores_done")
        s_logit = sem("logits_written")
        s_max = sem("neg_max_ready")
        s_exp = sem("exp_written")
        s_pt = sem("p_transposed")
        s_phi = sem("p_hi_written")
        s_plo = sem("p_lo_written")
        s_pv = sem("pv_done")
        s_half = sem("half_out_copied")
        s_sum = sem("row_sum_ready")
        s_inv = sem("inv_sum_ready")
        s_add = sem("halves_added")
        s_fin = sem("result_ready")

        def passed(eng):
            eng.sem_inc(s_passed, 1)

        block = ctx.enter_context(nc.Block())

        @block.sync
        def _(sp):
            def load_x_rows(g, b):
                sp.dma_start(x_rows[:, b], x_groups[g]).then_inc(s_x[b], 16)

            def spill_q(g, b):
                sp.wait_ge(s_qw, DB * g + DB)
                for k in range(DB):
                    sp.dma_start(q_spill[g, :, :, k, :].rearrange("j p q -> p j q"),
                                 q_out[:, b, k, :].rearrange("p (j q) -> p j q", j=GT)).then_inc(s_qst[b], 16)

            load_x_rows(0, 0)
            for n, w in enumerate((wq, wk, wv)):
                sp.dma_start(w_nat[:, n], w.rearrange("(o p) i -> p o i", p=P)).then_inc(s_w, 16)
            load_x_rows(1, 1)
            sp.dma_start(bq_col[:, :], bq.rearrange("(k p) -> p k", p=P), allow_slow_non_contiguous=True).then_inc(s_bias, 16)
            sp.dma_start(bk_col[:, :], bk.rearrange("(k p) -> p k", p=P), allow_slow_non_contiguous=True).then_inc(s_bias, 16)
            for n in range(2):
                sp.dma_start(bv_rows[:, n], bass.AP(bv.tensor, 0, [[0, P], [1, D]])).then_inc(s_bias, 16)

            sp.wait_ge(s_wt, 3)
            for n in range(QT):
                sp.dma_start(logits[:, 0, n * QC * BANK:(n + 1) * QC * BANK],
                             adj_tiles[0, :, n * QC * BANK:(n + 1) * QC * BANK]).then_inc(s_adj[0][n], 16)

            def prelude_step(g, b, spill=True, load=True):
                if load:
                    sp.wait_ge(s_ht, DB * g + DB)
                    load_x_rows(g + 2, b)
                if spill:
                    spill_q(g - 1, 1 - b)

            prelude_step(0, 0, spill=False)
            prelude_step(1, 1)
            with sp.Fori(1, GROUPS // 2 - 1) as i:
                prelude_step(2 * i, 0)
                prelude_step(2 * i + 1, 1)
            prelude_step(GROUPS - 2, 0, load=False)
            prelude_step(GROUPS - 1, 1, load=False)
            spill_q(GROUPS - 1, 1)

            def load_adj(t, b, n):
                sp.dma_start(logits[:, b, n * QC * BANK:(n + 1) * QC * BANK],
                             adj_tiles[t, :, n * QC * BANK:(n + 1) * QC * BANK]).then_inc(s_adj[b][n], 16)

            def load_q(t, b, group, j):
                sp.dma_start(q_raw[:, b], q_spill[group, j]).then_inc(s_qin[b], 16)

            def load_x_res(t, b):
                sp.dma_start(x_res[:, b], x_tiles[t]).then_inc(s_xr[b], 16)

            sp.wait_ge(s_vlo, 2 * GROUPS)
            sp.wait_ge(s_qst[0], 16 * DB * GROUPS // 2)
            sp.wait_ge(s_qst[1], 16 * DB * GROUPS // 2)
            q_tiles = q_spill.rearrange("g j p k q -> (g j) p k q")

            def load_q_tile(t, b):
                sp.dma_start(q_raw[:, b], q_tiles[t]).then_inc(s_qin[b], 16)

            load_q_tile(0, 0)
            load_q_tile(1, 1)
            sp.wait_ge(s_ht, DB * GROUPS)
            for n in range(QT):
                load_adj(1, 1, n)
            load_x_res(0, 0)
            load_x_res(1, 1)
            sp.wait_ge(s_qlo, 1)
            load_q_tile(2, 0)
            for n in range(QT):
                sp.wait_ge(s_pt, QC * (n + 1))
                load_adj(2, 0, n)

            def store(t, b):
                sp.wait_ge(s_fin, t + 1)
                sp.dma_start(out_tiles[t], x_res[:, b]).then_inc(s_out[b], 16)

            def main_step(t, i, b, fetch=True):
                store(t - 2, b)
                sp.wait_ge(s_out[b], 16 * i)
                load_x_res(t, b)
                if fetch:
                    sp.wait_ge(s_qlo, t)
                    load_q_tile(t + 1, 1 - b)
                    for n in range(QT):
                        sp.wait_ge(s_pt, CH * (t - 1) + QC * (n + 1))
                        load_adj(t + 1, 1 - b, n)

            with sp.Fori(1, TILES // 2 - 1) as i:
                main_step(2 * i, i, 0)
                main_step(2 * i + 1, i, 1)
            main_step(TILES - 2, TILES // 2 - 1, 0)
            main_step(TILES - 1, TILES // 2 - 1, 1, fetch=False)
            store(TILES - 2, 0)
            store(TILES - 1, 1)
            for b in range(2):
                sp.wait_ge(s_out[b], 16 * TILES // 2)

        @block.gpsimd
        def _(pool):
            nc.gpsimd.memset(ident[:, :], 0.0).then_inc(s_zero, 1)
            pool.wait_ge(s_zero, 1)
            nc.gpsimd.affine_select(out=ident[:, :], in_=ident[:, :], compare_op=ALU.not_equal, fill=1.0,
                                    base=0, pattern=[[-1, P]], channel_multiplier=1).then_inc(s_ident, 1)
            nc.gpsimd.memset(minus_half[:, :], -0.5).then_inc(s_const, 1)
            pool.wait_ge(s_const, 1)

            def make_rstd(g, b):
                pool.wait_ge(s_mv, g + 1)
                passed(pool)
                nc.gpsimd.tensor_scalar(var_eps[:, b], mean_var[:, b, :, 1], EPS, 1.0, ALU.add, ALU.mult)\
                    .then_inc(s_ve, 1)
                pool.wait_ge(s_ve, g + 1)
                nc.gpsimd.tensor_tensor(rstd[:, b], var_eps[:, b], minus_half[:, :], ALU.pow).then_inc(s_rstd, 1)

            def split_v(g):
                for j in range(2):
                    pool.wait_ge(s_vhi, 2 * g + j + 1)
                    at = v[:, bass.ds(GT * g + 2 * j, 2), :, :]
                    nc.gpsimd.tensor_tensor(at[:, :, 1, :], v_sum[:, j], at[:, :, 0, :].bitcast(f32),
                                            ALU.subtract).then_inc(s_vlo, 1)

            make_rstd(0, 0)
            make_rstd(1, 1)
            with pool.Fori(1, GROUPS // 2) as i:
                make_rstd(2 * i, 0)
                split_v(2 * i - 2)
                make_rstd(2 * i + 1, 1)
                split_v(2 * i - 1)
            split_v(GROUPS - 2)
            split_v(GROUPS - 1)

            def split_q(t, i, b, free=True):
                pool.wait_ge(s_qin[b], 16 * i + 16)
                if free:
                    pool.wait_ge(s_score, CH * (t - 1))
                passed(pool)
                nc.gpsimd.tensor_copy(qhl[:, b, 0], q_raw[:, b]).then_inc(s_qhi, 1)
                pool.wait_ge(s_qhi, t + 1)
                nc.gpsimd.tensor_tensor(qhl[:, b, 1], q_raw[:, b], qhl[:, b, 0].bitcast(f32),
                                        ALU.subtract).then_inc(s_qlo, 1)

            split_q(0, 0, 0, free=False)
            split_q(1, 0, 1, free=False)
            with pool.Fori(1, TILES // 2) as i:
                for b in range(2):
                    split_q(2 * i + b, i, b)

        @block.tensor
        def _(pe):
            pe.wait_ge(s_ident, 1)
            for w in range(3):
                pe.wait_ge(s_w, 16 * 3)
                for ib in range(DB):
                    for ob in range(DB):
                        last = nc.tensor.transpose(ps[:, w, ib * D + ob * P:ib * D + (ob + 1) * P],
                                                   w_nat[:, w, ob, ib * P:(ib + 1) * P], ident[:, :])
                last.then_inc(s_wt, 1)

            def transpose_h(g, b, first=False):
                pe.wait_ge(s_norm, g + 1)
                for ib in range(DB):
                    if not first:
                        pe.wait_ge(s_hlo, DB * (g - 1) + ib + 1)
                    for j in range(GT):
                        last = nc.tensor.transpose(ps[:, PT_BANK + ib, j * P:(j + 1) * P],
                                                   x_rows[:, b, j, ib * P:(ib + 1) * P], ident[:, :])
                    last.then_inc(s_ht, 1)

            def split_product(dst, lhs, rhs):
                n = 0
                for ib in range(DB):
                    for a, c in ((0, 0), (0, 1), (1, 0)):
                        last = nc.tensor.matmul(dst, lhs(a, ib), rhs(c, ib), start=(n == 0), stop=(n == 3 * DB - 1))
                        n += 1
                return last

            def project(g, b, first=False):
                pe.wait_ge(s_hlo, DB * g + DB)
                for ob in range(DB):
                    if not first:
                        pe.wait_ge(s_klo, DB * (g - 1) + ob + 1)
                    split_product(ps[:, ob, :], lambda a, ib: wT[:, 1, a, ib, ob * P:(ob + 1) * P],
                                  lambda c, ib: hT[:, b, c, ib, :]).then_inc(s_kmm, 1)
                for ob in range(DB):
                    if not first:
                        pe.wait_ge(s_qw, DB * (g - 1) + ob + 1)
                    split_product(ps[:, DB + ob, :], lambda a, ib: wT[:, 0, a, ib, ob * P:(ob + 1) * P],
                                  lambda c, ib: hT[:, b, c, ib, :]).then_inc(s_qmm, 1)
                for pair in range(2):
                    if not first:
                        pe.wait_ge(s_vs, 2 * (g - 1) + pair + 1)
                    for j in range(2):
                        r = (2 * pair + j) * P
                        last = split_product(ps[:, O_BANK + pair, j * D:(j + 1) * D],
                                             lambda a, ib: hT[:, b, a, ib, r:r + P],
                                             lambda c, ib: wT[:, 2, c, ib, :])
                    last.then_inc(s_vmm, 1)

            transpose_h(0, 0, first=True)
            transpose_h(1, 1)
            pe.wait_ge(s_wlo, 3)
            project(0, 0, first=True)
            with pe.Fori(1, GROUPS // 2) as i:
                transpose_h(2 * i, 0)
                project(2 * i - 1, 1)
                transpose_h(2 * i + 1, 1)
                project(2 * i, 0)
            project(GROUPS - 1, 1)

            def scores(t, b, c, free):
                if c == 0:
                    pe.wait_ge(s_qlo, t + 1)
                if free:
                    pe.wait_ge(s_logit, CH * t + c - SB + 1)
                split_product(ps[:, c % SB, :], lambda a, k: qhl[:, b, a, k, :],
                              lambda a, k: kT[:, a, k, c * BANK:(c + 1) * BANK]).then_inc(s_score, 1)

            def transpose_p(t, b, c, free):
                pe.wait_ge(s_exp, CH * t + c + 1)
                if free:
                    pe.wait_ge(s_plo, CH * t + c - 1)
                for k in range(KB):
                    last = nc.tensor.transpose(ps[:, PT_BANK + c % 2, k * P:(k + 1) * P],
                                               logits[:, b, c * BANK + k * P:c * BANK + (k + 1) * P], ident[:, :])
                last.then_inc(s_pt, 1)

            def weigh_values(t, b, c, free):
                if c == 0 and free:
                    pe.wait_ge(s_fin, t - 1)
                pe.wait_ge(s_plo, CH * t + c + 1)
                for k in range(KB):
                    n = KB * c + k
                    nc.tensor.matmul(ps[:, O_BANK + b, :], pT[:, c % 2, 0, k * P:(k + 1) * P],
                                     v[:, n, :, :].rearrange("p a d -> p (a d)"),
                                     start=(n == 0), stop=False)
                    last = nc.tensor.matmul(ps[:, O_BANK + b, 0:D], pT[:, c % 2, 1, k * P:(k + 1) * P],
                                            v[:, n, 0, :], start=False, stop=(n == TILES - 1))
                last.then_inc(s_pv, 1)

            pe.wait_ge(s_klo, DB * GROUPS)
            pe.wait_ge(s_qw, DB * GROUPS)
            pe.wait_ge(s_vlo, 2 * GROUPS)
            for c in range(CH):
                scores(0, 0, c, c >= SB)
            for c in range(CH):
                scores(1, 1, c, True)
                transpose_p(0, 0, c, c >= 2)
                if c > 0:
                    weigh_values(0, 0, c - 1, False)

            def main_step(t, b, free):
                for c in range(CH):
                    scores(t, b, c, True)
                    transpose_p(t - 1, 1 - b, c, True)
                    if c == 0:
                        weigh_values(t - 2, b, CH - 1, True)
                    else:
                        weigh_values(t - 1, 1 - b, c - 1, free)

            main_step(2, 0, False)
            main_step(3, 1, True)
            with pe.Fori(2, TILES // 2) as i:
                main_step(2 * i, 0, True)
                main_step(2 * i + 1, 1, True)
            for c in range(CH):
                transpose_p(TILES - 1, 1, c, True)
                if c == 0:
                    weigh_values(TILES - 2, 0, CH - 1, True)
                else:
                    weigh_values(TILES - 1, 1, c - 1, True)
            weigh_values(TILES - 1, 1, CH - 1, True)

        @block.scalar
        def _(act):
            act.wait_ge(s_zero, 1)
            act.wait_ge(s_bias, 16 * 4)
            nc.scalar.mul(bqs_col[:, :], bq_col[:, :], QSCALE).then_inc(s_bqs, 1)
            for w in range(3):
                act.wait_ge(s_wt, w + 1)
                nc.scalar.copy(wT[:, w, 0], ps[:, w, :].rearrange("p (i o) -> p i o", i=DB)).then_inc(s_whi, 1)
            act.wait_ge(s_bqs, 1)

            def h_hi(g, b, free):
                for ib in range(DB):
                    act.wait_ge(s_ht, DB * g + ib + 1)
                    if free and ib == 0:
                        act.wait_ge(s_vmm, 2 * (g - 1))
                    nc.scalar.activation(hT[:, b, 0, ib], ps[:, PT_BANK + ib, :], ACT.Relu).then_inc(s_hhi, 1)

            def project_hi(g, i, b, free):
                for ob in range(DB):
                    act.wait_ge(s_kmm, DB * g + ob + 1)
                    nc.scalar.activation(kT[:, 0, ob, bass.ds(g * BANK, BANK)], ps[:, ob, :], ACT.Identity,
                                         bias=bk_col[:, ob:ob + 1]).then_inc(s_khi, 1)
                for ob in range(DB):
                    act.wait_ge(s_qmm, DB * g + ob + 1)
                    if free and ob == 0:
                        act.wait_ge(s_qst[b], 16 * DB * i)
                    nc.scalar.activation(q_out[:, b, ob], ps[:, DB + ob, :], ACT.Identity,
                                         bias=bqs_col[:, ob:ob + 1], scale=QSCALE).then_inc(s_qw, 1)
                for j in range(2):
                    act.wait_ge(s_vs, 2 * g + j + 1)
                    nc.scalar.copy(v[:, bass.ds(GT * g + 2 * j, 2), 0, :], v_sum[:, j]).then_inc(s_vhi, 1)

            h_hi(0, 0, False)
            h_hi(1, 1, False)
            project_hi(0, 0, 0, False)
            h_hi(2, 0, True)
            project_hi(1, 0, 1, False)
            h_hi(3, 1, True)
            project_hi(2, 1, 0, True)
            with act.Fori(2, GROUPS // 2) as i:
                h_hi(2 * i, 0, True)
                project_hi(2 * i - 1, i - 1, 1, True)
                h_hi(2 * i + 1, 1, True)
                project_hi(2 * i, i, 0, True)
            project_hi(GROUPS - 1, GROUPS // 2 - 1, 1, True)

            def exponentials(t, b, c, free):
                if c == 0:
                    act.wait_ge(s_max, t + 1)
                    if free:
                        act.wait_ge(s_fin, t - 1)
                nc.scalar.activation(logits[:, b, c * BANK:(c + 1) * BANK], logits[:, b, c * BANK:(c + 1) * BANK],
                                     ACT.Exp, bias=neg_max[:, b:b + 1],
                                     accum_out=chunk_sum[:, b, c:c + 1]).then_inc(s_exp, 1)

            def p_hi(t, c, free):
                act.wait_ge(s_pt, CH * t + c + 1)
                if free:
                    act.wait_ge(s_pv, CH * t + c - 1)
                nc.scalar.copy(pT[:, c % 2, 0], ps[:, PT_BANK + c % 2, :]).then_inc(s_phi, 1)

            def copy_half(t, b, free):
                act.wait_ge(s_pv, CH * t + CH)
                if free:
                    act.wait_ge(s_fin, t - 1)
                nc.scalar.copy(half_out[:, b], ps[:, O_BANK + b, D:2 * D]).then_inc(s_half, 1)

            def main_step(t, b, free, half=True, half_free=True):
                exponentials(t, b, 0, free)
                for c in range(CH):
                    if c < CH - 1:
                        exponentials(t, b, c + 1, free)
                    if half and c == 1:
                        copy_half(t - 1, 1 - b, half_free)
                    p_hi(t, c, half or c >= 2)

            main_step(0, 0, False, half=False)
            main_step(1, 1, False, half_free=False)
            main_step(2, 0, True, half_free=False)
            main_step(3, 1, True)
            with act.Fori(2, TILES // 2) as i:
                main_step(2 * i, 0, True)
                main_step(2 * i + 1, 1, True)
            copy_half(TILES - 1, 1, True)

        @block.vector
        def _(dve):
            def group_stats(g, b):
                for j in range(GT):
                    nc.vector.bn_stats(stats[:, j], x_rows[:, b, j]).then_inc(s_stat, 1)
                dve.wait_ge(s_stat, GT * g + GT)
                passed(dve)
                for j in range(GT):
                    last = nc.vector.bn_aggr(mean_var[:, b, j], stats[:, j])
                last.then_inc(s_mv, 1)

            def normalize(g, b):
                dve.wait_ge(s_rstd, g + 1)
                for j in range(GT):
                    last = nc.vector.tensor_scalar(x_rows[:, b, j], x_rows[:, b, j], mean_var[:, b, j, 0:1],
                                                   rstd[:, b, j:j + 1], ALU.subtract, ALU.mult)
                last.then_inc(s_norm, 1)

            def h_lo(g, b):
                for ib in range(DB):
                    dve.wait_ge(s_hhi, DB * g + ib + 1)
                    nc.vector.scalar_tensor_tensor(hT[:, b, 1, ib], ps[:, PT_BANK + ib, :], 0.0,
                                                   hT[:, b, 0, ib].bitcast(f32), ALU.max,
                                                   ALU.subtract).then_inc(s_hlo, 1)

            def k_lo(g):
                for ob in range(DB):
                    dve.wait_ge(s_khi, DB * g + ob + 1)
                    nc.vector.scalar_tensor_tensor(kT[:, 1, ob, bass.ds(g * BANK, BANK)], ps[:, ob, :],
                                                   bk_col[:, ob:ob + 1],
                                                   kT[:, 0, ob, bass.ds(g * BANK, BANK)].bitcast(f32),
                                                   ALU.add, ALU.subtract).then_inc(s_klo, 1)

            def v_bias(g, free):
                for j in range(2):
                    dve.wait_ge(s_vmm, 2 * g + j + 1)
                    if free:
                        dve.wait_ge(s_vlo, 2 * (g - 1) + j + 1)
                    nc.vector.tensor_tensor(v_sum[:, j], ps[:, O_BANK + j, :].rearrange("p (j d) -> p j d", j=2),
                                            bv_rows, ALU.add).then_inc(s_vs, 1)

            def prelude_step(g, b, i_next, b_next, stat=True, first=False, free=True):
                if stat:
                    dve.wait_ge(s_x[b_next], 16 * i_next + 16)
                    group_stats(g + 1, b_next)
                h_lo(g, b)
                if stat:
                    normalize(g + 1, b_next)
                if not first:
                    k_lo(g - 1)
                    v_bias(g - 1, free)

            dve.wait_ge(s_x[0], 16)
            group_stats(0, 0)
            for w in range(3):
                dve.wait_ge(s_whi, w + 1)
                nc.vector.tensor_tensor(wT[:, w, 1], ps[:, w, :].rearrange("p (i o) -> p i o", i=DB),
                                        wT[:, w, 0].bitcast(f32), ALU.subtract).then_inc(s_wlo, 1)
            normalize(0, 0)
            dve.wait_ge(s_bias, 16 * 4)
            prelude_step(0, 0, 0, 1, first=True)
            prelude_step(1, 1, 1, 0, free=False)
            with dve.Fori(1, GROUPS // 2 - 1) as i:
                prelude_step(2 * i, 0, i, 1)
                prelude_step(2 * i + 1, 1, i + 1, 0)
            prelude_step(GROUPS - 2, 0, GROUPS // 2 - 1, 1)
            prelude_step(GROUPS - 1, 1, 0, 0, stat=False)
            k_lo(GROUPS - 1)
            v_bias(GROUPS - 1, True)

            def add_adj(t, i, b, c):
                dve.wait_ge(s_score, CH * t + c + 1)
                if c % QC == 0:
                    dve.wait_ge(s_adj[b][c // QC], 16 * i + 16)
                passed(dve)
                at = logits[:, b, c * BANK:(c + 1) * BANK]
                nc.vector.tensor_tensor_reduce(out=at, in0=ps[:, c % SB, :], in1=at, scale=2.0, scalar=LOWEST,
                                               op0=ALU.add, op1=ALU.max,
                                               accum_out=chunk_max[:, b, c:c + 1]).then_inc(s_logit, 1)

            def row_max(t, b, free):
                dve.wait_ge(s_logit, CH * t + CH)
                if free:
                    dve.wait_ge(s_exp, CH * (t - 1))
                nc.vector.tensor_reduce(out=neg_max[:, b:b + 1], in_=chunk_max[:, b], axis=AX.X, op=ALU.max,
                                        negate=True).then_inc(s_max, 1)

            def p_lo(t, c):
                dve.wait_ge(s_phi, CH * t + c + 1)
                nc.vector.tensor_tensor(pT[:, c % 2, 1], ps[:, PT_BANK + c % 2, :], pT[:, c % 2, 0].bitcast(f32),
                                        ALU.subtract).then_inc(s_plo, 1)

            def finish(t, i, b):
                dve.wait_ge(s_exp, CH * t + CH)
                nc.vector.reduce_sum(row_sum[:, :], chunk_sum[:, b], axis=AX.X).then_inc(s_sum, 1)
                dve.wait_ge(s_sum, t + 1)
                nc.vector.reciprocal(inv_sum[:, :], row_sum[:, :]).then_inc(s_inv, 1)
                dve.wait_ge(s_half, t + 1)
                nc.vector.tensor_tensor(half_out[:, b], ps[:, O_BANK + b, 0:D], half_out[:, b],
                                        ALU.add).then_inc(s_add, 1)
                dve.wait_ge(s_add, t + 1)
                dve.wait_ge(s_inv, t + 1)
                dve.wait_ge(s_xr[b], 16 * i + 16)
                nc.vector.scalar_tensor_tensor(x_res[:, b], half_out[:, b], inv_sum[:, :], x_res[:, b],
                                               ALU.mult, ALU.add).then_inc(s_fin, 1)

            for c in range(CH):
                add_adj(0, 0, 0, c)
            row_max(0, 0, False)
            for c in range(CH):
                add_adj(1, 0, 1, c)
                if c == CH - 1:
                    row_max(1, 1, False)
                p_lo(0, c)

            def main_step(t, i, i_fin, b):
                for c in range(CH):
                    add_adj(t, i, b, c)
                    if c == CH - 1:
                        row_max(t, b, True)
                    p_lo(t - 1, c)
                    if c == 1:
                        finish(t - 2, i_fin, b)

            with dve.Fori(1, TILES // 2) as i:
                main_step(2 * i, i, i - 1, 0)
                main_step(2 * i + 1, i, i - 1, 1)
            for c in range(CH):
                p_lo(TILES - 1, c)
                if c == 1:
                    finish(TILES - 2, TILES // 2 - 1, 0)
            finish(TILES - 1, TILES // 2 - 1, 1)


_INS = ["x", "adj", "L0_gnn_Wq", "L0_gnn_bq", "L0_gnn_Wk", "L0_gnn_bk", "L0_gnn_Wv", "L0_gnn_bv"]


def kernel(**inputs):
    import numpy as np
    import concourse.bacc as bacc
    from concourse.bass_utils import run_bass_kernel_spmd

    nc = bacc.Bacc("TRN2", target_bir_lowering=False, num_devices=1)
    arrays, args = {}, []
    for name in _INS:
        a = np.ascontiguousarray(inputs[name])
        arrays[f"in_{name}"] = a
        args.append(nc.dram_tensor(f"in_{name}", a.shape, mybir.dt.from_np(a.dtype), kind="ExternalInput").ap())
    out = nc.dram_tensor("out", inputs["x"].shape, mybir.dt.float32, kind="ExternalOutput").ap()
    graph_attention_kernel(nc, *args, out)
    result = run_bass_kernel_spmd(nc, [arrays], core_ids=[0])
    return result.results[0]["out"]
```

```python
import concourse.bass as bass
from concourse import mybir
from contextlib import ExitStack


def graph_attention_kernel(nc, x, adj, wq, bq, wk, bk, wv, bv, out):
    f32 = mybir.dt.float32
    f32r = mybir.dt.float32r
    ALU = mybir.AluOpType
    ACT = mybir.ActivationFunctionType
    AX = mybir.AxisListType

    P = 128
    Q = 32
    QN = P // Q
    N, D = x.shape
    DB = D // P
    BANK = 512
    TILES = N // P
    CH = N // BANK
    KB = BANK // P
    GROUPS = N // BANK
    GT = BANK // P
    CLS = N // QN
    CC = CLS // BANK
    SB = 4
    EPS = 1e-5
    QSCALE = 0.5 * float(D) ** -0.5
    LOWEST = -3.4028234663852886e38

    x_groups = x.rearrange("(c g j i) d -> g c i j d", c=QN, g=GROUPS, j=GT)
    x_tiles = x.rearrange("(t p) d -> t p d", p=P)
    out_tiles = out.rearrange("(t p) d -> t p d", p=P)
    adj_tiles = adj.rearrange("(t p) n -> t p n", p=P)

    ctx = ExitStack()
    with ctx:
        def sb(name, shape, dt=f32, within=ctx):
            return within.enter_context(nc.sbuf_tensor(name, shape, dt))

        def sem(name):
            return ctx.enter_context(nc.semaphore(name))

        q_spill = nc.dram_tensor("q_spill", [DB, P, N], f32, kind="Internal").ap()
        q_groups = q_spill.rearrange("k p (c g r) -> g k p c r", c=QN, g=GROUPS)
        q_tiles = q_spill.rearrange("k p (t q) -> t p k q", q=P)

        kT = sb("kT", [P, 2, DB, N], f32r)
        v = sb("v", [P, TILES, 2, D], f32r)
        logits = sb("logits", [P, 2, N])
        qhl = sb("qhl", [P, 2, 2, DB, P], f32r)
        q_raw = sb("q_raw", [P, DB, P])
        x_res = sb("x_res", [P, D])
        half_out = sb("half_out", [P, D])
        bq_col = sb("bq_col", [P, DB])
        bqs_col = sb("bqs_col", [P, DB])
        bk_col = sb("bk_col", [P, DB])
        chunk_max = sb("chunk_max", [P, 2, CH])
        neg_max = sb("neg_max", [P, 2])
        chunk_sum = sb("chunk_sum", [P, 2, CH])
        row_sum = sb("row_sum", [P, 1])
        inv_sum = sb("inv_sum", [P, 1])

        w_nat = logits[:, 0, 0:3 * DB * D].rearrange("p (w o i) -> p w o i", w=3, o=DB)
        x_rows = logits[:, 1, 0:2 * GT * D].rearrange("p (b j d) -> p b j d", b=2, j=GT)
        q_out = logits[:, 1, 2 * GT * D:2 * GT * D + 2 * DB * BANK]\
            .rearrange("p (b k r) -> p b k r", b=2, k=DB)
        with ExitStack() as prelude:
            wT = sb("wT", [P, 3, 2, DB, D], f32r, prelude)
            hT = sb("hT", [P, 2, 2, DB, BANK], f32r, prelude)
            v_sum = sb("v_sum", [P, 2, 2, D], f32, prelude)
            bv_rows = sb("bv_rows", [P, 2, D], f32, prelude)
            ident = sb("ident", [P, P], f32, prelude)
            stats = sb("stats", [P, GT, 6], f32, prelude)
            mean_var = sb("mean_var", [P, 2, GT, 2], f32, prelude)
            var_eps = sb("var_eps", [P, 2, GT], f32, prelude)
            minus_half = sb("minus_half", [P, GT], f32, prelude)
            rstd = sb("rstd", [P, 2, GT], f32, prelude)
        landed = sb("landed", [P, 2, QN, CLS])
        pT = sb("pT", [P, 2, 2, BANK], f32r)

        ps = ctx.enter_context(nc.psum_tensor("ps", [P, 8, BANK], f32))
        HT_BANK, O_BANK = 4, 6

        s_passed = sem("waits_passed")
        s_w = sem("w_loaded")
        s_bias = sem("bias_loaded")
        s_x = [sem(f"x_rows_loaded{b}") for b in range(2)]
        s_adj = [[sem(f"adj_loaded{b}_{n}") for n in range(QN)] for b in range(2)]
        s_xr = sem("x_res_loaded")
        s_qin = sem("q_loaded")
        s_qst = [sem(f"q_spilled{b}") for b in range(2)]
        s_out = sem("out_stored")
        s_zero = sem("ident_zeroed")
        s_ident = sem("ident_made")
        s_const = sem("constants_made")
        s_wt = sem("w_transposed")
        s_whi = sem("w_hi_written")
        s_wlo = sem("w_lo_written")
        s_bqs = sem("bq_scaled")
        s_stat = sem("bn_stats_done")
        s_mv = sem("mean_var_ready")
        s_ve = sem("var_eps_ready")
        s_rstd = sem("rstd_ready")
        s_norm = sem("x_normalized")
        s_ht = sem("h_transposed")
        s_hhi = sem("h_hi_written")
        s_hlo = sem("h_lo_written")
        s_kmm = sem("k_projected")
        s_qmm = sem("q_projected")
        s_vmm = sem("v_projected")
        s_khi = sem("k_hi_written")
        s_klo = sem("k_lo_written")
        s_qw = sem("q_written")
        s_vs = sem("v_biased")
        s_vhi = sem("v_hi_written")
        s_vlo = sem("v_lo_written")
        s_qhi = sem("q_hi_written")
        s_qlo = sem("q_lo_written")
        s_score = sem("scores_done")
        s_logit = sem("logits_written")
        s_max = sem("neg_max_ready")
        s_exp = sem("exp_written")
        s_blk = sem("blocks_transposed")
        s_land = [[sem(f"class_landed{b}_{n}") for n in range(QN)] for b in range(2)]
        s_phi = sem("p_hi_written")
        s_plo = sem("p_lo_written")
        s_pv = sem("pv_done")
        s_half = sem("half_out_copied")
        s_sum = sem("row_sum_ready")
        s_inv = sem("inv_sum_ready")
        s_add = sem("halves_added")
        s_fin = sem("result_ready")

        def passed(eng):
            eng.sem_inc(s_passed, 1)

        block = ctx.enter_context(nc.Block())

        @block.sync
        def _(sp):
            def load_x_rows(g, b):
                for c in range(QN):
                    sp.dma_start(x_rows[c * Q:(c + 1) * Q, b], x_groups[g, c]).then_inc(s_x[b], 16)

            def spill_q(g, b):
                sp.wait_ge(s_qw, DB * g + DB)
                for k in range(DB):
                    sp.dma_start(q_groups[g, k], q_out[:, b, k, :].rearrange("p (c r) -> p c r", c=QN))\
                        .then_inc(s_qst[b], 16)

            def load_adj(t, b, n):
                sp.dma_start(logits[:, b, n * CLS:(n + 1) * CLS],
                             adj_tiles[t, :, n * CLS:(n + 1) * CLS]).then_inc(s_adj[b][n], 16)

            for n, w in enumerate((wq, wk, wv)):
                sp.dma_start(w_nat[:, n], w.rearrange("(o p) i -> p o i", p=P)).then_inc(s_w, 16)
            load_x_rows(0, 0)
            load_x_rows(1, 1)
            sp.dma_start(bq_col[:, :], bq.rearrange("(k p) -> p k", p=P),
                         allow_slow_non_contiguous=True).then_inc(s_bias, 16)
            sp.dma_start(bk_col[:, :], bk.rearrange("(k p) -> p k", p=P),
                         allow_slow_non_contiguous=True).then_inc(s_bias, 16)
            for n in range(2):
                sp.dma_start(bv_rows[:, n], bass.AP(bv.tensor, 0, [[0, P], [1, D]])).then_inc(s_bias, 16)
            sp.wait_ge(s_wt, 3)
            for n in range(QN):
                load_adj(0, 0, n)

            def prelude_step(g, b, spill=True, load=True):
                if load:
                    sp.wait_ge(s_ht, DB * g + DB)
                    load_x_rows(g + 2, b)
                if spill:
                    spill_q(g - 1, 1 - b)

            prelude_step(0, 0, spill=False)
            prelude_step(1, 1)
            with sp.Fori(1, GROUPS // 2 - 1) as i:
                prelude_step(2 * i, 0)
                prelude_step(2 * i + 1, 1)
            prelude_step(GROUPS - 2, 0, load=False)
            prelude_step(GROUPS - 1, 1, load=False)
            sp.wait_ge(s_ht, DB * GROUPS)
            sp.wait_ge(s_qst[0], 16 * DB * GROUPS // 2)
            for n in range(QN // 2):
                load_adj(1, 1, n)
            spill_q(GROUPS - 1, 1)
            sp.wait_ge(s_qst[1], 16 * DB * GROUPS // 2)
            for n in range(QN // 2, QN):
                load_adj(1, 1, n)

            def exchange(t, b, c, free):
                sp.wait_ge(s_blk, QN * t + c + 1)
                passed(sp)
                if c == 0 and free:
                    sp.wait_ge(s_plo, CH * (t - 1))
                for a in range(QN):
                    sp.dma_start(landed[c * Q:(c + 1) * Q, b, a, :],
                                 logits[a * Q:(a + 1) * Q, b, c * CLS:(c + 1) * CLS]).then_inc(s_land[b][c], 16)

            def period(t, i, b, fetch=True, free=True):
                for c in range(QN):
                    exchange(t - 1, 1 - b, c, free)
                    if fetch and c > 0:
                        sp.wait_ge(s_land[1 - b][c - 1], 16 * QN * i + 16 * QN)
                        passed(sp)
                        load_adj(t + 1, 1 - b, c - 1)
                if fetch:
                    sp.wait_ge(s_land[1 - b][QN - 1], 16 * QN * i + 16 * QN)
                    passed(sp)
                    load_adj(t + 1, 1 - b, QN - 1)

            period(1, 0, 1, free=False)
            period(2, 0, 0, free=False)
            period(3, 1, 1)
            with sp.Fori(2, TILES // 2 - 1) as i:
                period(2 * i, i - 1, 0)
                period(2 * i + 1, i, 1)
            period(TILES - 2, TILES // 2 - 2, 0)
            period(TILES - 1, 0, 1, fetch=False)
            period(TILES, 0, 0, fetch=False)

        @block.gpsimd
        def _(pool):
            nc.gpsimd.memset(ident[:, :], 0.0).then_inc(s_zero, 1)
            pool.wait_ge(s_zero, 1)
            nc.gpsimd.affine_select(out=ident[:, :], in_=ident[:, :], compare_op=ALU.not_equal, fill=1.0,
                                    base=0, pattern=[[-1, P]], channel_multiplier=1).then_inc(s_ident, 1)
            nc.gpsimd.memset(minus_half[:, :], -0.5).then_inc(s_const, 1)
            pool.wait_ge(s_const, 1)

            def make_rstd(g, b):
                pool.wait_ge(s_mv, g + 1)
                passed(pool)
                nc.gpsimd.tensor_scalar(var_eps[:, b], mean_var[:, b, :, 1], EPS, 1.0, ALU.add, ALU.mult)\
                    .then_inc(s_ve, 1)
                pool.wait_ge(s_ve, g + 1)
                nc.gpsimd.tensor_tensor(rstd[:, b], var_eps[:, b], minus_half[:, :], ALU.pow).then_inc(s_rstd, 1)

            def split_v(g):
                for j in range(2):
                    pool.wait_ge(s_vhi, 2 * g + j + 1)
                    at = v[:, bass.ds(GT * g + 2 * j, 2), :, :]
                    nc.gpsimd.tensor_tensor(at[:, :, 1, :], v_sum[:, j], at[:, :, 0, :].bitcast(f32),
                                            ALU.subtract).then_inc(s_vlo, 1)

            make_rstd(0, 0)
            make_rstd(1, 1)
            with pool.Fori(1, GROUPS // 2) as i:
                make_rstd(2 * i, 0)
                split_v(2 * i - 2)
                make_rstd(2 * i + 1, 1)
                split_v(2 * i - 1)

            def load_q(t):
                pool.dma_start(q_raw[:, :, :], q_tiles[t]).then_inc(s_qin, 16)

            def split_q(t, b, free=True):
                pool.wait_ge(s_qin, 16 * t + 16)
                if free:
                    pool.wait_ge(s_score, CH * (t - 1))
                passed(pool)
                nc.gpsimd.tensor_copy(qhl[:, b, 0], q_raw[:, :, :]).then_inc(s_qhi, 1)
                pool.wait_ge(s_qhi, t + 1)
                nc.gpsimd.tensor_tensor(qhl[:, b, 1], q_raw[:, :, :], qhl[:, b, 0].bitcast(f32),
                                        ALU.subtract).then_inc(s_qlo, 1)

            def load_x_res(t):
                pool.dma_start(x_res[:, :], x_tiles[t]).then_inc(s_xr, 16)

            def store(t):
                pool.wait_ge(s_fin, t + 1)
                passed(pool)
                pool.dma_start(out_tiles[t], x_res[:, :]).then_inc(s_out, 16)
                pool.wait_ge(s_out, 16 * t + 16)
                passed(pool)

            pool.wait_ge(s_qst[0], 16 * DB)
            load_q(0)
            split_q(0, 0, free=False)
            split_v(GROUPS - 2)
            pool.wait_ge(s_qlo, 1)
            load_q(1)
            split_v(GROUPS - 1)
            load_x_res(0)

            split_q(1, 1, free=False)
            for t in (1, 2, 3):
                pool.wait_ge(s_qlo, t + 1)
                load_q(t + 1)
                split_q(t + 1, (t + 1) % 2)
                if t == 3:
                    store(0)
                    load_x_res(1)

            def main_period(t, b):
                pool.wait_ge(s_qlo, t + 1)
                passed(pool)
                load_q(t + 1)
                split_q(t + 1, 1 - b)
                store(t - 3)
                load_x_res(t - 2)

            with pool.Fori(2, TILES // 2 - 1) as i:
                main_period(2 * i, 0)
                main_period(2 * i + 1, 1)
            main_period(TILES - 2, 0)
            for t in (TILES - 1, TILES, TILES + 1):
                store(t - 3)
                load_x_res(t - 2)
            store(TILES - 1)

        @block.tensor
        def _(pe):
            pe.wait_ge(s_ident, 1)
            for w in range(3):
                pe.wait_ge(s_w, 16 * 3)
                for ib in range(DB):
                    for ob in range(DB):
                        last = nc.tensor.transpose(ps[:, w, ib * D + ob * P:ib * D + (ob + 1) * P],
                                                   w_nat[:, w, ob, ib * P:(ib + 1) * P], ident[:, :])
                last.then_inc(s_wt, 1)

            def transpose_h(g, b, first=False):
                pe.wait_ge(s_norm, g + 1)
                for ib in range(DB):
                    if not first:
                        pe.wait_ge(s_hlo, DB * (g - 1) + ib + 1)
                    for j in range(GT):
                        last = nc.tensor.transpose(ps[:, HT_BANK + ib, j * P:(j + 1) * P],
                                                   x_rows[:, b, j, ib * P:(ib + 1) * P], ident[:, :])
                    last.then_inc(s_ht, 1)

            def split_product(dst, lhs, rhs):
                n = 0
                for ib in range(DB):
                    for a, c in ((0, 0), (0, 1), (1, 0)):
                        last = nc.tensor.matmul(dst, lhs(a, ib), rhs(c, ib), start=(n == 0), stop=(n == 3 * DB - 1))
                        n += 1
                return last

            def project(g, b, first=False):
                def in_order(c, ib):
                    return hT[:, b, c, ib, :].rearrange("p (j c i) -> p c j i", c=QN, j=GT)

                pe.wait_ge(s_hlo, DB * g + DB)
                for ob in range(DB):
                    if not first:
                        pe.wait_ge(s_klo, DB * (g - 1) + ob + 1)
                    split_product(ps[:, ob, :], lambda a, ib: wT[:, 1, a, ib, ob * P:(ob + 1) * P],
                                  in_order).then_inc(s_kmm, 1)
                for ob in range(DB):
                    if not first:
                        pe.wait_ge(s_qw, DB * (g - 1) + ob + 1)
                    split_product(ps[:, DB + ob, :], lambda a, ib: wT[:, 0, a, ib, ob * P:(ob + 1) * P],
                                  in_order).then_inc(s_qmm, 1)
                for pair in range(2):
                    if not first:
                        pe.wait_ge(s_vs, 2 * (g - 1) + pair + 1)
                    for n in range(2):
                        j = 2 * pair + n
                        last = split_product(
                            ps[:, O_BANK + pair, n * D:(n + 1) * D],
                            lambda a, ib: hT[:, b, a, ib, j * P:(j + 1) * P],
                            lambda c, ib: wT[:, 2, c, ib, :])
                    last.then_inc(s_vmm, 1)

            transpose_h(0, 0, first=True)
            transpose_h(1, 1)
            pe.wait_ge(s_wlo, 3)
            project(0, 0, first=True)
            with pe.Fori(1, GROUPS // 2) as i:
                transpose_h(2 * i, 0)
                project(2 * i - 1, 1)
                transpose_h(2 * i + 1, 1)
                project(2 * i, 0)
            project(GROUPS - 1, 1)

            def scores(t, b, c, free):
                if c == 0:
                    pe.wait_ge(s_qlo, t + 1)
                if free:
                    pe.wait_ge(s_logit, CH * t + c - SB + 1)
                split_product(ps[:, c % SB, :], lambda a, k: qhl[:, b, a, k, :],
                              lambda a, k: kT[:, a, k, c * BANK:(c + 1) * BANK]).then_inc(s_score, 1)

            def weigh_values(t, b, c, free):
                if c == 0 and free:
                    pe.wait_ge(s_fin, t - 1)
                pe.wait_ge(s_plo, CH * t + c + 1)
                for k in range(KB):
                    n = KB * c + k
                    nc.tensor.matmul(ps[:, O_BANK + b, :], pT[:, c % 2, 0, k * P:(k + 1) * P],
                                     v[:, n, :, :].rearrange("p a d -> p (a d)"),
                                     start=(n == 0), stop=False)
                    last = nc.tensor.matmul(ps[:, O_BANK + b, 0:D], pT[:, c % 2, 1, k * P:(k + 1) * P],
                                            v[:, n, 0, :], start=False, stop=(n == TILES - 1))
                last.then_inc(s_pv, 1)

            def period(t, b, free=True):
                for c in range(CH):
                    scores(t, b, c, True)
                    weigh_values(t - 2, b, c, free)

            pe.wait_ge(s_klo, DB * GROUPS)
            pe.wait_ge(s_qw, DB * GROUPS)
            pe.wait_ge(s_vlo, 2 * GROUPS)
            for c in range(CH):
                scores(0, 0, c, c >= SB)
            for c in range(CH):
                scores(1, 1, c, True)
            period(2, 0, free=False)
            period(3, 1, free=False)
            with pe.Fori(2, TILES // 2) as i:
                period(2 * i, 0)
                period(2 * i + 1, 1)
            for c in range(CH):
                weigh_values(TILES - 2, 0, c, True)
            for c in range(CH):
                weigh_values(TILES - 1, 1, c, True)

        @block.scalar
        def _(act):
            for w in range(3):
                act.wait_ge(s_wt, w + 1)
                nc.scalar.copy(wT[:, w, 0], ps[:, w, :].rearrange("p (i o) -> p i o", i=DB)).then_inc(s_whi, 1)

            def h_hi(g, b, free):
                for ib in range(DB):
                    act.wait_ge(s_ht, DB * g + ib + 1)
                    if free and ib == 0:
                        act.wait_ge(s_vmm, 2 * (g - 1))
                    nc.scalar.activation(hT[:, b, 0, ib], ps[:, HT_BANK + ib, :], ACT.Relu).then_inc(s_hhi, 1)

            def project_hi(g, i, b, free):
                for ob in range(DB):
                    act.wait_ge(s_kmm, DB * g + ob + 1)
                    nc.scalar.activation(
                        kT[:, 0, ob, :].rearrange("p (c r) -> p c r", c=QN)[:, :, bass.ds(g * P, P)],
                        ps[:, ob, :].rearrange("p (c r) -> p c r", c=QN), ACT.Identity,
                        bias=bk_col[:, ob:ob + 1]).then_inc(s_khi, 1)
                for ob in range(DB):
                    act.wait_ge(s_qmm, DB * g + ob + 1)
                    if free and ob == 0:
                        act.wait_ge(s_qst[b], 16 * DB * i)
                    nc.scalar.activation(q_out[:, b, ob], ps[:, DB + ob, :], ACT.Identity,
                                         bias=bqs_col[:, ob:ob + 1], scale=QSCALE).then_inc(s_qw, 1)
                for j in range(2):
                    act.wait_ge(s_vs, 2 * g + j + 1)
                    nc.scalar.copy(v[:, bass.ds(GT * g + 2 * j, 2), 0, :], v_sum[:, j]).then_inc(s_vhi, 1)

            h_hi(0, 0, False)
            act.wait_ge(s_bias, 16 * 4)
            nc.scalar.mul(bqs_col[:, :], bq_col[:, :], QSCALE).then_inc(s_bqs, 1)
            act.wait_ge(s_bqs, 1)
            h_hi(1, 1, False)
            project_hi(0, 0, 0, False)
            h_hi(2, 0, True)
            project_hi(1, 0, 1, False)
            h_hi(3, 1, True)
            project_hi(2, 1, 0, True)
            with act.Fori(2, GROUPS // 2) as i:
                h_hi(2 * i, 0, True)
                project_hi(2 * i - 1, i - 1, 1, True)
                h_hi(2 * i + 1, 1, True)
                project_hi(2 * i, i, 0, True)
            project_hi(GROUPS - 1, GROUPS // 2 - 1, 1, True)

            def exponentials(t, b, c, free):
                if c == 0:
                    act.wait_ge(s_max, t + 1)
                    if free:
                        act.wait_ge(s_sum, t - 1)
                nc.scalar.activation(logits[:, b, c * BANK:(c + 1) * BANK], logits[:, b, c * BANK:(c + 1) * BANK],
                                     ACT.Exp, bias=neg_max[:, b:b + 1],
                                     accum_out=chunk_sum[:, b, c:c + 1]).then_inc(s_exp, 1)

            def p_hi(t, i, b, c, free):
                if c == 0:
                    for n in range(QN):
                        act.wait_ge(s_land[b][n], 16 * QN * i + 16 * QN)
                if free:
                    act.wait_ge(s_pv, CH * t + c - 1)
                nc.scalar.copy(pT[:, c % 2, 0].rearrange("p (k a q) -> p k a q", k=KB, a=QN),
                               landed[:, b, :, c * P:(c + 1) * P].rearrange("p a (k q) -> p k a q", k=KB))\
                    .then_inc(s_phi, 1)

            def copy_half(t, b):
                act.wait_ge(s_pv, CH * t + CH)
                if not isinstance(t, int) or t > 0:
                    act.wait_ge(s_fin, t)
                nc.scalar.copy(half_out[:, :], ps[:, O_BANK + b, D:2 * D]).then_inc(s_half, 1)

            def period(t, i, b, soft=True, values=True, fin=True, exp_free=True, first=False):
                for c in range(CH):
                    if fin and c == 0:
                        copy_half(t - 3, 1 - b)
                    if soft and c < QN:
                        for n in range(CC):
                            exponentials(t - 1, 1 - b, CC * c + n, exp_free)
                    if values and c < CH - 1:
                        p_hi(t - 2, i - 1, b, c + 1, not first or c >= 1)
                    if soft and c == CH - 1:
                        p_hi(t - 1, i if b else i - 1, 1 - b, 0, values)

            period(1, 0, 1, values=False, fin=False, exp_free=False)
            period(2, 1, 0, fin=False, exp_free=False, first=True)
            period(3, 1, 1)
            with act.Fori(2, TILES // 2) as i:
                period(2 * i, i, 0)
                period(2 * i + 1, i, 1)
            period(TILES, TILES // 2, 0)
            period(TILES + 1, TILES // 2, 1, soft=False)
            copy_half(TILES - 1, 1)

        @block.vector
        def _(dve):
            def group_stats(g, b):
                for j in range(GT):
                    nc.vector.bn_stats(stats[:, j], x_rows[:, b, j]).then_inc(s_stat, 1)
                dve.wait_ge(s_stat, GT * g + GT)
                passed(dve)
                for j in range(GT):
                    last = nc.vector.bn_aggr(mean_var[:, b, j], stats[:, j])
                last.then_inc(s_mv, 1)

            def normalize(g, b):
                dve.wait_ge(s_rstd, g + 1)
                for j in range(GT):
                    last = nc.vector.tensor_scalar(x_rows[:, b, j], x_rows[:, b, j], mean_var[:, b, j, 0:1],
                                                   rstd[:, b, j:j + 1], ALU.subtract, ALU.mult)
                last.then_inc(s_norm, 1)

            def h_lo(g, b):
                for ib in range(DB):
                    dve.wait_ge(s_hhi, DB * g + ib + 1)
                    nc.vector.scalar_tensor_tensor(hT[:, b, 1, ib], ps[:, HT_BANK + ib, :], 0.0,
                                                   hT[:, b, 0, ib].bitcast(f32), ALU.max,
                                                   ALU.subtract).then_inc(s_hlo, 1)

            def k_lo(g):
                for ob in range(DB):
                    dve.wait_ge(s_khi, DB * g + ob + 1)
                    hi, lo = (kT[:, a, ob, :].rearrange("p (c r) -> p c r", c=QN)[:, :, bass.ds(g * P, P)]
                              for a in range(2))
                    nc.vector.scalar_tensor_tensor(lo, ps[:, ob, :].rearrange("p (c r) -> p c r", c=QN),
                                                   bk_col[:, ob:ob + 1], hi.bitcast(f32),
                                                   ALU.add, ALU.subtract).then_inc(s_klo, 1)

            def v_bias(g, free):
                for j in range(2):
                    dve.wait_ge(s_vmm, 2 * g + j + 1)
                    if free:
                        dve.wait_ge(s_vlo, 2 * (g - 1) + j + 1)
                    nc.vector.tensor_tensor(v_sum[:, j], ps[:, O_BANK + j, :].rearrange("p (j d) -> p j d", j=2),
                                            bv_rows[:, :, :], ALU.add).then_inc(s_vs, 1)

            def prelude_step(g, b, i_next, b_next, stat=True, first=False, free=True):
                if stat:
                    dve.wait_ge(s_x[b_next], 16 * QN * i_next + 16 * QN)
                    group_stats(g + 1, b_next)
                h_lo(g, b)
                if stat:
                    normalize(g + 1, b_next)
                if not first:
                    k_lo(g - 1)
                    v_bias(g - 1, free)

            dve.wait_ge(s_x[0], 16 * QN)
            group_stats(0, 0)
            for w in range(3):
                dve.wait_ge(s_whi, w + 1)
                nc.vector.tensor_tensor(wT[:, w, 1], ps[:, w, :].rearrange("p (i o) -> p i o", i=DB),
                                        wT[:, w, 0].bitcast(f32), ALU.subtract).then_inc(s_wlo, 1)
            normalize(0, 0)
            prelude_step(0, 0, 0, 1, first=True)
            dve.wait_ge(s_bias, 16 * 4)
            prelude_step(1, 1, 1, 0, free=False)
            with dve.Fori(1, GROUPS // 2 - 1) as i:
                prelude_step(2 * i, 0, i, 1)
                prelude_step(2 * i + 1, 1, i + 1, 0)
            prelude_step(GROUPS - 2, 0, GROUPS // 2 - 1, 1)
            prelude_step(GROUPS - 1, 1, 0, 0, stat=False)
            k_lo(GROUPS - 1)
            v_bias(GROUPS - 1, True)

            def add_adj(t, i, b, c):
                dve.wait_ge(s_score, CH * t + c + 1)
                if c % CC == 0:
                    dve.wait_ge(s_adj[b][c // CC], 16 * i + 16)
                passed(dve)
                at = logits[:, b, c * BANK:(c + 1) * BANK]
                nc.vector.tensor_tensor_reduce(out=at, in0=ps[:, c % SB, :], in1=at, scale=2.0, scalar=LOWEST,
                                               op0=ALU.add, op1=ALU.max,
                                               accum_out=chunk_max[:, b, c:c + 1]).then_inc(s_logit, 1)

            def row_max(t, b, free):
                dve.wait_ge(s_logit, CH * t + CH)
                if free:
                    dve.wait_ge(s_exp, CH * (t - 1))
                nc.vector.tensor_reduce(out=neg_max[:, b:b + 1], in_=chunk_max[:, b], axis=AX.X, op=ALU.max,
                                        negate=True).then_inc(s_max, 1)

            def transpose_blocks(t, b, c):
                dve.wait_ge(s_exp, CH * t + CC * c + CC)
                at = logits[:, b, c * CLS:(c + 1) * CLS]
                nc.vector.transpose(at, at).then_inc(s_blk, 1)

            def p_lo(t, b, c):
                dve.wait_ge(s_phi, CH * t + c + 1)
                nc.vector.tensor_tensor(pT[:, c % 2, 1].rearrange("p (k a q) -> p k a q", k=KB, a=QN),
                                        landed[:, b, :, c * P:(c + 1) * P].rearrange("p a (k q) -> p k a q", k=KB),
                                        pT[:, c % 2, 0].bitcast(f32).rearrange("p (k a q) -> p k a q", k=KB, a=QN),
                                        ALU.subtract).then_inc(s_plo, 1)

            def invert_sum(t, b):
                dve.wait_ge(s_exp, CH * t + CH)
                nc.vector.reduce_sum(row_sum[:, :], chunk_sum[:, b], axis=AX.X).then_inc(s_sum, 1)
                dve.wait_ge(s_sum, t + 1)
                nc.vector.reciprocal(inv_sum[:, :], row_sum[:, :]).then_inc(s_inv, 1)

            def finish(t, b):
                dve.wait_ge(s_half, t + 1)
                nc.vector.tensor_tensor(half_out[:, :], ps[:, O_BANK + b, 0:D], half_out[:, :],
                                        ALU.add).then_inc(s_add, 1)
                dve.wait_ge(s_add, t + 1)
                dve.wait_ge(s_inv, t + 1)
                dve.wait_ge(s_xr, 16 * t + 16)
                nc.vector.scalar_tensor_tensor(x_res[:, :], half_out[:, :], inv_sum[:, :], x_res[:, :],
                                               ALU.mult, ALU.add).then_inc(s_fin, 1)

            def period(t, i, b, score=True, soft=True, values=True, fin=True):
                for c in range(CH):
                    if score:
                        add_adj(t, i, b, c)
                        if c == CH - 1:
                            row_max(t, b, values)
                    if soft and 1 <= c <= QN:
                        transpose_blocks(t - 1, 1 - b, c - 1)
                    if values and c < CH - 1:
                        p_lo(t - 2, b, c + 1)
                    if soft and c == CH - 1:
                        p_lo(t - 1, 1 - b, 0)
                    if fin and c == 1:
                        finish(t - 3, 1 - b)
                    if values and c == 2:
                        invert_sum(t - 2, b)

            for c in range(CH):
                add_adj(0, 0, 0, c)
            row_max(0, 0, False)
            period(1, 0, 1, values=False, fin=False)
            period(2, 1, 0, fin=False)
            period(3, 1, 1)
            with dve.Fori(2, TILES // 2) as i:
                period(2 * i, i, 0)
                period(2 * i + 1, i, 1)
            period(TILES, TILES // 2, 0, score=False)
            period(TILES + 1, TILES // 2, 1, score=False, soft=False)
            finish(TILES - 1, 1)


_INS = ["x", "adj", "L0_gnn_Wq", "L0_gnn_bq", "L0_gnn_Wk", "L0_gnn_bk", "L0_gnn_Wv", "L0_gnn_bv"]


def kernel(**inputs):
    import numpy as np
    import concourse.bacc as bacc
    from concourse.bass_utils import run_bass_kernel_spmd

    nc = bacc.Bacc("TRN2", target_bir_lowering=False, num_devices=1)
    arrays, args = {}, []
    for name in _INS:
        a = np.ascontiguousarray(inputs[name])
        arrays[f"in_{name}"] = a
        args.append(nc.dram_tensor(f"in_{name}", a.shape, mybir.dt.from_np(a.dtype), kind="ExternalInput").ap())
    out = nc.dram_tensor("out", inputs["x"].shape, mybir.dt.float32, kind="ExternalOutput").ap()
    graph_attention_kernel(nc, *args, out)
    result = run_bass_kernel_spmd(nc, [arrays], core_ids=[0])
    return result.results[0]["out"]
```

```python
import concourse.bass as bass
from concourse import mybir
from contextlib import ExitStack


def graph_attention_kernel(nc, x, adj, wq, bq, wk, bk, wv, bv, out):
    f32 = mybir.dt.float32
    f32r = mybir.dt.float32r
    ALU = mybir.AluOpType
    ACT = mybir.ActivationFunctionType
    AX = mybir.AxisListType

    P = 128
    Q = 32
    QN = P // Q
    N, D = x.shape
    DB = D // P
    BANK = 512
    TILES = N // P
    CH = N // BANK
    KB = BANK // P
    GROUPS = N // BANK
    GT = BANK // P
    CLS = N // QN
    CC = CLS // BANK
    SB = 4
    EPS = 1e-5
    QSCALE = 0.5 * float(D) ** -0.5
    LOWEST = -3.4028234663852886e38

    x_groups = x.rearrange("(c g j i) d -> g c i j d", c=QN, g=GROUPS, j=GT)
    x_tiles = x.rearrange("(t p) d -> t p d", p=P)
    out_tiles = out.rearrange("(t p) d -> t p d", p=P)
    adj_tiles = adj.rearrange("(t p) n -> t p n", p=P)

    ctx = ExitStack()
    with ctx:
        def sb(name, shape, dt=f32, within=ctx):
            return within.enter_context(nc.sbuf_tensor(name, shape, dt))

        def sem(name):
            return ctx.enter_context(nc.semaphore(name))

        q_spill = nc.dram_tensor("q_spill", [DB, P, N], f32, kind="Internal").ap()
        q_groups = q_spill.rearrange("k p (c g r) -> g k p c r", c=QN, g=GROUPS)
        q_tiles = q_spill.rearrange("k p (t q) -> t p k q", q=P)
        term_spill = [nc.dram_tensor(f"term_spill{n}", [N], f32, kind="Internal").ap() for n in range(2)]
        term_tiles = [d.rearrange("(t p one) -> t p one", p=P, one=1) for d in term_spill]

        hT = sb("hT", [P, 2, DB, N], f32r)
        v = sb("v", [P, TILES, 2, D], f32r)
        logits = sb("logits", [P, 2, N])
        qhl = sb("qhl", [P, 2, 2, DB, P], f32r)
        q_raw = sb("q_raw", [P, DB, P])
        rows = sb("rows", [P, 2, D])
        x_res, half_out = rows[:, 0], rows[:, 1]
        bq_col = sb("bq_col", [P, DB])
        bk_pair = sb("bk_pair", [P, DB, 2])
        row_term = sb("row_term", [P, 2])
        minus_max = sb("minus_max", [P, 1])
        chunk_max = sb("chunk_max", [P, 2, CH])
        neg_max = sb("neg_max", [P, 2])
        chunk_sum = sb("chunk_sum", [P, 2, CH])
        row_sum = sb("row_sum", [P, 1])
        inv_sum = sb("inv_sum", [P, 2])

        w_nat = logits[:, 0, 0:3 * DB * D].rearrange("p (w o i) -> p w o i", w=3, o=DB)
        x_rows = logits[:, 1, 0:2 * GT * D].rearrange("p (b j d) -> p b j d", b=2, j=GT)
        q_out = logits[:, 1, 2 * GT * D:2 * GT * D + 2 * DB * BANK]\
            .rearrange("p (b k r) -> p b k r", b=2, k=DB)
        bv_rows = rows
        with ExitStack() as prelude:
            v_sum = sb("v_sum", [P, 2, 2, D], f32, prelude)
            wv_T = sb("wv_T", [P, 2, DB, D + 2], f32r, prelude)
            G = sb("G", [P, 2, DB, D], f32r, prelude)
            wqk = sb("wqk", [P, 2, 2, DB, D], f32r, prelude)
            ident = sb("ident", [P, P], f32, prelude)
            ones = sb("ones", [P, P], f32, prelude)
            stats = sb("stats", [P, GT, 6], f32, prelude)
            mean_var = sb("mean_var", [P, 2, GT, 2], f32, prelude)
            var_eps = sb("var_eps", [P, 2, GT], f32, prelude)
            minus_half = sb("minus_half", [P, GT], f32, prelude)
            rstd = sb("rstd", [P, 2, GT], f32, prelude)
            bias_products = sb("bias_products", [P, DB], f32, prelude)
            query_bias = sb("query_bias", [P, DB], f32, prelude)
            term_bias = sb("term_bias", [P, 1], f32, prelude)
            row_terms = sb("row_terms", [P, TILES], f32, prelude)
            terms_turned = sb("terms_turned", [P, 2, Q], f32, prelude)
        pT = sb("pT", [P, 2, 2, BANK], f32r)
        landed_1 = sb("landed_1", [P, QN, CLS])
        landed_0 = sb("landed_0", [P, QN, CLS])
        landed = [landed_0, landed_1]

        ps = ctx.enter_context(nc.psum_tensor("ps", [P, 8, BANK], f32))
        Q_BANK, HT_BANK, O_BANK = 2, 4, 6
        V_BANKS = (0, 6)
        WV_BANK, G_BANK, BIAS_BANK = 3, 6, 7

        def last_place(n):
            q_place = qhl.rearrange("p b a k q -> p (b a k q)").rearrange("p (a n) -> p a n", a=2)
            return (pT[:, 0] if n < 3 else q_place, pT[:, 1], pT[:, 0])[n % 3]

        s_passed = sem("waits_passed")
        s_w = [sem(f"w_loaded{n}") for n in range(3)]
        s_bias = sem("bias_loaded")
        s_x = [sem(f"x_rows_loaded{b}") for b in range(2)]
        s_adj = [[sem(f"adj_loaded{b}_{n}") for n in range(QN)] for b in range(2)]
        s_xr = sem("x_res_loaded")
        s_qin = sem("q_loaded")
        s_tin = [sem(f"row_term_loaded{b}") for b in range(2)]
        s_qst = [sem(f"q_spilled{b}") for b in range(2)]
        s_tst = [sem(f"row_terms_spilled{n}") for n in range(2)]
        s_out = sem("out_stored")
        s_last = sem("last_out_stored")
        s_zero = sem("ident_zeroed")
        s_ident = sem("ident_made")
        s_const = sem("constants_made")
        s_wt = sem("wv_transposed")
        s_whi = sem("wv_hi_written")
        s_wlo = sem("wv_lo_written")
        s_nhi = sem("wq_wk_hi_written")
        s_nlo = sem("wq_wk_lo_written")
        s_g = sem("G_done")
        s_ghi = sem("G_hi_written")
        s_glo = sem("G_lo_written")
        s_pad = sem("bk_zeros_written")
        s_bb = sem("bias_products_ready")
        s_bmm = sem("bias_terms_done")
        s_bcol = sem("bias_columns_ready")
        s_ulo = sem("wq_bk_lo_written")
        s_stat = sem("bn_stats_done")
        s_mv = sem("mean_var_ready")
        s_ve = sem("var_eps_ready")
        s_rstd = sem("rstd_ready")
        s_norm = sem("x_normalized")
        s_ht = sem("h_transposed")
        s_hhi = sem("h_hi_written")
        s_hlo = sem("h_lo_written")
        s_qmm = sem("q_projected")
        s_vmm = sem("v_projected")
        s_term = sem("row_terms_written")
        s_turn = sem("row_terms_turned")
        s_qw = sem("q_written")
        s_vs = sem("v_biased")
        s_vhi = sem("v_hi_written")
        s_vlo = sem("v_lo_written")
        s_qhi = sem("q_hi_written")
        s_qlo = sem("q_lo_written")
        s_score = sem("scores_done")
        s_logit = sem("logits_written")
        s_rmax = sem("minus_max_ready")
        s_max = sem("neg_max_ready")
        s_exp = sem("exp_written")
        s_blk = sem("blocks_transposed")
        s_land = [[sem(f"class_landed{b}_{n}") for n in range(QN)] for b in range(2)]
        s_phi = sem("p_hi_written")
        s_plo = sem("p_lo_written")
        s_pv = sem("pv_done")
        s_half = sem("half_out_copied")
        s_sum = sem("row_sum_ready")
        s_inv = sem("inv_sum_ready")
        s_add = sem("halves_added")
        s_fin = sem("result_ready")

        def passed(eng):
            eng.sem_inc(s_passed, 1)

        block = ctx.enter_context(nc.Block())

        @block.sync
        def _(sp):
            def load_x_rows(g, b):
                for c in range(QN):
                    sp.dma_start(x_rows[c * Q:(c + 1) * Q, b], x_groups[g, c]).then_inc(s_x[b], 16)

            def spill_q(g, b):
                sp.wait_ge(s_qw, DB * g + DB)
                for k in range(DB):
                    sp.dma_start(q_groups[g, k], q_out[:, b, k, :].rearrange("p (c r) -> p c r", c=QN))\
                        .then_inc(s_qst[b], 16)

            def spill_terms(n):
                sp.wait_ge(s_turn, n + 1)
                sp.dma_start(term_spill[n].rearrange("(p i) -> p i", p=P), terms_turned[:, n])\
                    .then_inc(s_tst[n], 16)

            def load_adj(t, b, n):
                sp.dma_start(logits[:, b, n * CLS:(n + 1) * CLS],
                             adj_tiles[t, :, n * CLS:(n + 1) * CLS]).then_inc(s_adj[b][n], 16)

            load_x_rows(0, 0)
            for n, w in enumerate((wq, wk, wv)):
                sp.dma_start(w_nat[:, n], w.rearrange("(o p) i -> p o i", p=P)).then_inc(s_w[n], 16)
            sp.dma_start(bq_col[:, :], bq.rearrange("(k p) -> p k", p=P),
                         allow_slow_non_contiguous=True).then_inc(s_bias, 16)
            sp.wait_ge(s_pad, 1)
            sp.dma_start(bk_pair[:, :, 0], bk.rearrange("(k p) -> p k", p=P),
                         allow_slow_non_contiguous=True).then_inc(s_bias, 16)
            for n in range(2):
                sp.dma_start(bv_rows[:, n], bass.AP(bv.tensor, 0, [[0, P], [1, D]])).then_inc(s_bias, 16)
            load_x_rows(1, 1)

            def prelude_step(g, b, spill=True, load=True):
                if load:
                    sp.wait_ge(s_ht, DB * g + DB)
                    load_x_rows(g + 2, b)
                if spill:
                    spill_q(g - 1, 1 - b)

            prelude_step(0, 0, spill=False)
            prelude_step(1, 1)
            sp.wait_ge(s_wt, 1)
            sp.wait_ge(s_nlo, 2)
            sp.wait_ge(s_bmm, 1)
            for n in range(QN // 2):
                load_adj(0, 0, n)
            with sp.Fori(1, GROUPS // 2 - 1) as i:
                prelude_step(2 * i, 0)
                prelude_step(2 * i + 1, 1)
            for n in range(QN // 2, QN):
                load_adj(0, 0, n)
            prelude_step(GROUPS - 2, 0, load=False)
            prelude_step(GROUPS - 1, 1, load=False)
            spill_terms(0)
            sp.wait_ge(s_ht, DB * GROUPS)
            sp.wait_ge(s_qst[0], 16 * DB * GROUPS // 2)
            for n in range(QN // 2):
                load_adj(1, 1, n)

            def exchange(t, b, c, free):
                sp.wait_ge(s_blk, QN * t + c + 1)
                passed(sp)
                if c == 0 and free:
                    sp.wait_ge(s_plo, CH * (t - 1))
                for a in range(QN):
                    sp.dma_start(landed[b][c * Q:(c + 1) * Q, a, :],
                                 logits[a * Q:(a + 1) * Q, b, c * CLS:(c + 1) * CLS]).then_inc(s_land[b][c], 16)

            def period(t, i, b, fetch=True, free=True):
                for c in range(QN):
                    exchange(t - 1, 1 - b, c, free)
                    if fetch and c > 0:
                        sp.wait_ge(s_land[1 - b][c - 1], 16 * QN * i + 16 * QN)
                        passed(sp)
                        load_adj(t + 1, 1 - b, c - 1)
                if fetch:
                    sp.wait_ge(s_land[1 - b][QN - 1], 16 * QN * i + 16 * QN)
                    passed(sp)
                    load_adj(t + 1, 1 - b, QN - 1)

            spill_q(GROUPS - 1, 1)
            exchange(0, 0, 0, False)
            sp.wait_ge(s_qst[1], 16 * DB * GROUPS // 2)
            for n in range(QN // 2, QN):
                load_adj(1, 1, n)
            for c in range(1, QN):
                exchange(0, 0, c, False)
            spill_terms(1)
            sp.wait_ge(s_tst[1], 16)
            for c in range(QN):
                sp.wait_ge(s_land[0][c], 16 * QN)
                load_adj(2, 0, c)
            period(2, 0, 0, free=False)
            period(3, 1, 1)
            with sp.Fori(2, TILES // 2 - 1) as i:
                period(2 * i, i - 1, 0)
                period(2 * i + 1, i, 1)
            period(TILES - 2, TILES // 2 - 2, 0)
            period(TILES - 1, 0, 1, fetch=False)
            period(TILES, 0, 0, fetch=False)
            sp.wait_ge(s_fin, TILES)
            sp.dma_start(out_tiles[TILES - 1], x_res).then_inc(s_last, 16)
            sp.wait_ge(s_last, 16)

        @block.gpsimd
        def _(pool):
            nc.gpsimd.memset(ident[:, :], 0.0).then_inc(s_zero, 1)
            pool.wait_ge(s_zero, 1)
            nc.gpsimd.affine_select(out=ident[:, :], in_=ident[:, :], compare_op=ALU.not_equal, fill=1.0,
                                    base=0, pattern=[[-1, P]], channel_multiplier=1).then_inc(s_ident, 1)
            nc.gpsimd.memset(bk_pair[:, :, :], 0.0).then_inc(s_pad, 1)
            nc.gpsimd.memset(row_terms[:, :], 0.0)
            nc.gpsimd.memset(ones[:, :], 1.0)
            nc.gpsimd.memset(minus_half[:, :], -0.5).then_inc(s_const, 1)
            pool.wait_ge(s_const, 1)

            def make_rstd(g, b):
                pool.wait_ge(s_mv, g + 1)
                passed(pool)
                nc.gpsimd.tensor_scalar(var_eps[:, b], mean_var[:, b, :, 1], EPS, 1.0, ALU.add, ALU.mult)\
                    .then_inc(s_ve, 1)
                pool.wait_ge(s_ve, g + 1)
                nc.gpsimd.tensor_tensor(rstd[:, b], var_eps[:, b], minus_half[:, :], ALU.pow).then_inc(s_rstd, 1)

            def split_v(g, pairs=(0, 1)):
                for j in pairs:
                    pool.wait_ge(s_vhi, 2 * g + j + 1)
                    at = v[:, bass.ds(GT * g + 2 * j, 2), :, :]
                    nc.gpsimd.tensor_tensor(at[:, :, 1, :], v_sum[:, j], at[:, :, 0, :].bitcast(f32),
                                            ALU.subtract).then_inc(s_vlo, 1)

            make_rstd(0, 0)
            make_rstd(1, 1)
            make_rstd(2, 0)
            make_rstd(3, 1)
            split_v(0)
            with pool.Fori(2, GROUPS // 2 - 1) as i:
                split_v(2 * i - 3, (0,))
                make_rstd(2 * i, 0)
                split_v(2 * i - 3, (1,))
                split_v(2 * i - 2, (0,))
                make_rstd(2 * i + 1, 1)
                split_v(2 * i - 2, (1,))

            def load_q(t):
                pool.dma_start(q_raw[:, :, :], q_tiles[t]).then_inc(s_qin, 16)

            def split_q(t, b, free=True):
                pool.wait_ge(s_qin, 16 * t + 16)
                if free:
                    pool.wait_ge(s_score, CH * (t - 1))
                passed(pool)
                nc.gpsimd.tensor_copy(qhl[:, b, 0], q_raw[:, :, :]).then_inc(s_qhi, 1)
                pool.wait_ge(s_qhi, t + 1)
                nc.gpsimd.tensor_tensor(qhl[:, b, 1], q_raw[:, :, :], qhl[:, b, 0].bitcast(f32),
                                        ALU.subtract).then_inc(s_qlo, 1)

            def load_term(t, b, n):
                pool.dma_start(row_term[:, b:b + 1], term_tiles[n][t], allow_slow_non_contiguous=True)\
                    .then_inc(s_tin[b], 16)

            def load_x_res(t):
                pool.dma_start(x_res, x_tiles[t]).then_inc(s_xr, 16)

            def store(t):
                pool.wait_ge(s_fin, t + 1)
                passed(pool)
                pool.dma_start(out_tiles[t], x_res).then_inc(s_out, 16)
                pool.wait_ge(s_out, 16 * t + 16)
                passed(pool)

            pool.wait_ge(s_qst[0], 16 * DB)
            load_q(0)
            split_v(GROUPS - 5, (0,))
            make_rstd(GROUPS - 2, 0)
            split_v(GROUPS - 5, (1,))
            split_q(0, 0, free=False)
            pool.wait_ge(s_qlo, 1)
            pool.wait_ge(s_qst[1], 16 * DB)
            load_q(1)
            split_v(GROUPS - 4, (0,))
            make_rstd(GROUPS - 1, 1)
            split_v(GROUPS - 4, (1,))
            split_v(GROUPS - 3)
            split_q(1, 1, free=False)
            pool.wait_ge(s_tst[0], 16)
            load_term(0, 0, 0)
            load_term(1, 1, 0)
            split_v(GROUPS - 2)
            split_v(GROUPS - 1)
            pool.wait_ge(s_vs, 2 * GROUPS)
            load_x_res(0)
            for t in (1, 2, 3):
                pool.wait_ge(s_qlo, t + 1)
                load_q(t + 1)
                split_q(t + 1, (t + 1) % 2)
                pool.wait_ge(s_max, t)
                load_term(t + 1, (t + 1) % 2, 0)
                if t == 3:
                    store(0)
                    load_x_res(1)

            pool.wait_ge(s_tst[1], 16)

            def main_period(t, b):
                pool.wait_ge(s_qlo, t + 1)
                passed(pool)
                load_q(t + 1)
                split_q(t + 1, 1 - b)
                pool.wait_ge(s_max, t)
                passed(pool)
                load_term(t + 1, 1 - b, 1)
                store(t - 3)
                load_x_res(t - 2)

            with pool.Fori(2, TILES // 2 - 1) as i:
                main_period(2 * i, 0)
                main_period(2 * i + 1, 1)
            main_period(TILES - 2, 0)
            for t in (TILES - 1, TILES, TILES + 1):
                store(t - 3)
                load_x_res(t - 2)

        @block.tensor
        def _(pe):
            pe.wait_ge(s_ident, 1)
            pe.wait_ge(s_w[2], 16)
            for ib in range(DB):
                for ob in range(DB):
                    last = nc.tensor.transpose(ps[:, WV_BANK, ib * D + ob * P:ib * D + (ob + 1) * P],
                                               w_nat[:, 2, ob, ib * P:(ib + 1) * P], ident[:, :])
            last.then_inc(s_wt, 1)

            def transpose_h(g, b, first=False):
                pe.wait_ge(s_norm, g + 1)
                for ib in range(DB):
                    if not first:
                        pe.wait_ge(s_hlo, DB * (g - 1) + ib + 1)
                    for j in range(GT):
                        last = nc.tensor.transpose(ps[:, HT_BANK + ib, j * P:(j + 1) * P],
                                                   x_rows[:, b, j, ib * P:(ib + 1) * P], ident[:, :])
                    last.then_inc(s_ht, 1)

            def split_product(dst, lhs, rhs):
                n = 0
                for ib in range(DB):
                    for a, c in ((0, 0), (0, 1), (1, 0)):
                        last = nc.tensor.matmul(dst, lhs(a, ib), rhs(c, ib), start=(n == 0), stop=(n == 3 * DB - 1))
                        n += 1
                return last

            def multiply_weights():
                pe.wait_ge(s_nlo, 2)
                for m in range(DB):
                    last = split_product(ps[:, G_BANK, m * D:(m + 1) * D],
                                         lambda a, ob: wqk[:, 0, a, ob, m * P:(m + 1) * P],
                                         lambda a, ob: wqk[:, 1, a, ob, :])
                last.then_inc(s_g, 1)
                pe.wait_ge(s_bb, 1)
                for m in range(DB):
                    for ob in range(DB):
                        nc.tensor.matmul(ps[:, BIAS_BANK, 2 * m:2 * m + 2], w_nat[:, 0, ob, m * P:(m + 1) * P],
                                         bk_pair[:, ob, :], start=(ob == 0), stop=(ob == DB - 1))
                for m in range(DB):
                    for ob in range(DB):
                        nc.tensor.matmul(ps[:, BIAS_BANK, 2 * DB + m:2 * DB + m + 1],
                                         w_nat[:, 1, ob, m * P:(m + 1) * P],
                                         bq_col[:, ob:ob + 1], start=(ob == 0), stop=(ob == DB - 1))
                for ob in range(DB):
                    last = nc.tensor.matmul(ps[:, BIAS_BANK, 3 * DB:3 * DB + 1], ones[:, :],
                                            bias_products[:, ob:ob + 1], start=(ob == 0), stop=(ob == DB - 1))
                last.then_inc(s_bmm, 1)

            def project_q(g, first=False, bank=Q_BANK):
                pe.wait_ge(s_hlo, DB * g + DB)
                for ob in range(DB):
                    if not first:
                        pe.wait_ge(s_qw, DB * (g - 1) + ob + 1)
                    elif ob == 0:
                        pe.wait_ge(s_glo, 1)
                    split_product(ps[:, bank + ob, :], lambda a, ib: G[:, a, ib, ob * P:(ob + 1) * P],
                                  lambda a, ib: hT[:, a, ib, bass.ds(g * BANK, BANK)]
                                  .rearrange("p (j c i) -> p c j i", c=QN, j=GT)).then_inc(s_qmm, 1)

            def project_v(g, first=False, scored=0):
                for pair in range(2):
                    if not first:
                        pe.wait_ge(s_vs, 2 * (g - 1) + pair + 1)
                    elif pair == 0:
                        pe.wait_ge(s_wlo, 1)
                        pe.wait_ge(s_ulo, 1)
                        pe.wait_ge(s_glo, 1)
                        pe.wait_ge(s_bcol, 1)
                    if scored and pair == 0:
                        pe.wait_ge(s_logit, scored)
                    for n in range(2):
                        last = split_product(
                            ps[:, V_BANKS[pair] + n, 0:D + 2],
                            lambda a, ib: hT[:, a, ib, bass.ds(g * BANK + (2 * pair + n) * P, P)],
                            lambda c, ib: wv_T[:, c, ib, :])
                    last.then_inc(s_vmm, 1)

            transpose_h(0, 0, first=True)
            multiply_weights()
            transpose_h(1, 1)
            pe.wait_ge(s_wlo, 1)
            project_q(0, first=True)
            project_v(0, first=True)
            for g in range(2, GROUPS - 1):
                transpose_h(g, g % 2)
                project_q(g - 1)
                project_v(g - 1)
            transpose_h(GROUPS - 1, 1)
            project_q(GROUPS - 2)

            def scores(t, b, c, free):
                if c == 0:
                    pe.wait_ge(s_qlo, t + 1)
                if free:
                    pe.wait_ge(s_logit, CH * t + c - SB + 1)
                keys = hT.rearrange("p a k (B c i) -> p a k B c i", c=QN, i=Q)
                blocks = slice(c % CC * (BANK // Q), (c % CC + 1) * (BANK // Q))
                split_product(ps[:, c % SB, :], lambda a, k: qhl[:, b, a, k, :],
                              lambda a, k: keys[:, a, k, blocks, c // CC, :]).then_inc(s_score, 1)

            def weigh_values(t, b, c, free, place=None):
                place = pT[:, c % 2] if place is None else place
                if c == 0 and free:
                    pe.wait_ge(s_fin, t - 1)
                pe.wait_ge(s_plo, CH * t + c + 1)
                for k in range(KB):
                    n = KB * c + k
                    nc.tensor.matmul(ps[:, O_BANK + b, :], place[:, 0, k * P:(k + 1) * P],
                                     v[:, n, :, :].rearrange("p a d -> p (a d)"),
                                     start=(n == 0), stop=False)
                    last = nc.tensor.matmul(ps[:, O_BANK + b, 0:D], place[:, 1, k * P:(k + 1) * P],
                                            v[:, n, 0, :], start=False, stop=(n == TILES - 1))
                last.then_inc(s_pv, 1)

            def period(t, b, free=True):
                for c in range(CH):
                    scores(t, b, c, True)
                    weigh_values(t - 2, b, c, free)

            pe.wait_ge(s_hlo, DB * GROUPS)
            pe.wait_ge(s_vs, 2 * (GROUPS - 3) + 1)
            for c in range(CH):
                if Q_BANK <= c < Q_BANK + DB:
                    pe.wait_ge(s_qw, DB * (GROUPS - 2) + c - Q_BANK + 1)
                scores(0, 0, c, c >= SB)
            project_q(GROUPS - 1, bank=HT_BANK)
            project_v(GROUPS - 2, scored=CH - SB + 2)
            project_v(GROUPS - 1)
            pe.wait_ge(s_vs, 2 * GROUPS - 1)
            for c in range(CH):
                scores(1, 1, c, True)
            pe.wait_ge(s_vlo, 2 * GROUPS)
            period(2, 0, free=False)
            period(3, 1, free=False)
            with pe.Fori(2, TILES // 2 - 1) as i:
                period(2 * i, 0)
                period(2 * i + 1, 1)
            period(TILES - 2, 0)
            for c in range(CH - 1):
                scores(TILES - 1, 1, c, True)
            weigh_values(TILES - 3, 1, 0, True, last_place(0))
            scores(TILES - 1, 1, CH - 1, True)
            for n in range(1, 3 * CH):
                t = TILES - 3 + n // CH
                weigh_values(t, t % 2, n % CH, True, last_place(n))

        @block.scalar
        def _(act):
            for w in range(2):
                act.wait_ge(s_w[w], 16)
                nc.scalar.copy(wqk[:, w, 0], w_nat[:, w]).then_inc(s_nhi, 1)
            act.wait_ge(s_wt, 1)
            nc.scalar.copy(wv_T[:, 0, :, 0:D], ps[:, WV_BANK, :].rearrange("p (i o) -> p i o", i=DB))\
                .then_inc(s_whi, 1)

            def h_hi(g):
                for ib in range(DB):
                    act.wait_ge(s_ht, DB * g + ib + 1)
                    nc.scalar.activation(hT[:, 0, ib, bass.ds(g * BANK, BANK)], ps[:, HT_BANK + ib, :],
                                         ACT.Relu).then_inc(s_hhi, 1)

            def write_q(g, i, b, free, bank=Q_BANK):
                for ob in range(DB):
                    act.wait_ge(s_qmm, DB * g + ob + 1)
                    if free and ob == 0:
                        act.wait_ge(s_qst[b], 16 * DB * i)
                    nc.scalar.activation(q_out[:, b, ob], ps[:, bank + ob, :], ACT.Identity,
                                         bias=query_bias[:, ob:ob + 1], scale=QSCALE).then_inc(s_qw, 1)

            def v_hi(g):
                for j in range(2):
                    act.wait_ge(s_vs, 2 * g + j + 1)
                    nc.scalar.copy(v[:, bass.ds(GT * g + 2 * j, 2), 0, :], v_sum[:, j]).then_inc(s_vhi, 1)

            h_hi(0)
            act.wait_ge(s_g, 1)
            nc.scalar.copy(G[:, 0], ps[:, G_BANK, :].rearrange("p (i o) -> p i o", i=DB)).then_inc(s_ghi, 1)
            act.wait_ge(s_bmm, 1)
            nc.scalar.copy(wv_T[:, 0, :, D:D + 2], ps[:, BIAS_BANK, 0:2 * DB].rearrange("p (i n) -> p i n", n=2))
            nc.scalar.mul(query_bias[:, :], ps[:, BIAS_BANK, 2 * DB:3 * DB], QSCALE)
            nc.scalar.copy(term_bias[:, :], ps[:, BIAS_BANK, 3 * DB:3 * DB + 1]).then_inc(s_bcol, 1)
            act.wait_ge(s_bcol, 1)
            h_hi(1)
            write_q(0, 0, 0, False)
            v_hi(0)
            h_hi(2)
            write_q(1, 0, 1, False)
            v_hi(1)
            h_hi(3)
            write_q(2, 1, 0, True)
            v_hi(2)
            with act.Fori(2, GROUPS // 2 - 1) as i:
                h_hi(2 * i)
                write_q(2 * i - 1, i - 1, 1, True)
                v_hi(2 * i - 1)
                h_hi(2 * i + 1)
                write_q(2 * i, i, 0, True)
                v_hi(2 * i)
            h_hi(GROUPS - 2)
            write_q(GROUPS - 3, GROUPS // 2 - 2, 1, True)
            h_hi(GROUPS - 1)
            v_hi(GROUPS - 3)
            write_q(GROUPS - 2, GROUPS // 2 - 1, 0, True)

            def exponentials(t, b, n, free):
                if n == 0:
                    act.wait_ge(s_max, t + 1)
                    if free:
                        act.wait_ge(s_sum, t - 1)
                for c in range(CC * n, CC * n + CC):
                    at = logits[:, b, c * BANK:(c + 1) * BANK]
                    nc.scalar.activation(at, at, ACT.Exp, bias=neg_max[:, b:b + 1],
                                         accum_out=chunk_sum[:, b, c:c + 1]).then_inc(s_exp, 1)

            def copy_p_hi(b, c, place):
                nc.scalar.copy(place[:, 0].rearrange("p (k a q) -> p k a q", k=KB, a=QN),
                               landed[b][:, :, c * P:(c + 1) * P].rearrange("p a (k q) -> p k a q", k=KB))\
                    .then_inc(s_phi, 1)

            def p_hi(t, i, b, c, free):
                if c == 0:
                    for n in range(QN):
                        act.wait_ge(s_land[b][n], 16 * QN * i + 16 * QN)
                if free:
                    act.wait_ge(s_pv, CH * t + c - 1)
                copy_p_hi(b, c, pT[:, c % 2])

            def copy_half(t, b):
                act.wait_ge(s_pv, CH * t + CH)
                if not isinstance(t, int) or t > 0:
                    act.wait_ge(s_fin, t)
                nc.scalar.copy(half_out, ps[:, O_BANK + b, D:2 * D]).then_inc(s_half, 1)

            def period(t, i, b, soft=True, values=True, fin_at=4, exp_free=True, first=False):
                for c in range(CH):
                    if values and c < CH - 1:
                        p_hi(t - 2, i - 1, b, c + 1, not first or c >= 1)
                    if soft and c < QN:
                        exponentials(t - 1, 1 - b, c, exp_free)
                    if c == fin_at:
                        copy_half(t - 3, 1 - b)
                    if soft and c == CH - 1:
                        p_hi(t - 1, i if b else i - 1, 1 - b, 0, values)

            exponentials(0, 0, 0, False)
            write_q(GROUPS - 1, GROUPS // 2 - 1, 1, True, HT_BANK)
            exponentials(0, 0, 1, False)
            v_hi(GROUPS - 2)
            exponentials(0, 0, 2, False)
            exponentials(0, 0, 3, False)
            v_hi(GROUPS - 1)
            act.wait_ge(s_vlo, 2 * GROUPS)
            p_hi(0, 0, 0, 0, False)
            period(2, 1, 0, fin_at=None, exp_free=False, first=True)
            period(3, 1, 1)
            with act.Fori(2, TILES // 2 - 1) as i:
                period(2 * i, i, 0)
                period(2 * i + 1, i, 1)
            t, i = TILES - 1, TILES // 2 - 1
            period(t - 1, i, 0)

            def last_p_hi(n):
                if n == 3:
                    act.wait_ge(s_score, CH * TILES)
                if n % CH == 0:
                    for m in range(QN):
                        act.wait_ge(s_land[(n // CH + 1) % 2][m], 16 * QN * (TILES // 2))
                act.wait_ge(s_pv, CH * (t - 2) + max(n - 2, min(n - 1, 1)))
                copy_p_hi((n // CH + 1) % 2, n % CH, last_place(n))

            last_p_hi(1)
            for n in range(QN):
                exponentials(t - 1, 0, n, True)
            copy_half(t - 3, 0)
            for n in range(2, 3 * CH):
                last_p_hi(n)
                if n % 2 == 1 and n // 2 - 1 < QN:
                    exponentials(t, 1, n // 2 - 1, True)
                if n % CH == 1:
                    copy_half(t - 3 + n // CH, (n // CH) % 2)
            copy_half(t, 1)

        @block.vector
        def _(dve):
            def group_stats(g, b):
                for j in range(GT):
                    nc.vector.bn_stats(stats[:, j], x_rows[:, b, j]).then_inc(s_stat, 1)
                dve.wait_ge(s_stat, GT * g + GT)
                passed(dve)
                for j in range(GT):
                    last = nc.vector.bn_aggr(mean_var[:, b, j], stats[:, j])
                last.then_inc(s_mv, 1)

            def normalize(g, b):
                dve.wait_ge(s_rstd, g + 1)
                for j in range(GT):
                    last = nc.vector.tensor_scalar(x_rows[:, b, j], x_rows[:, b, j], mean_var[:, b, j, 0:1],
                                                   rstd[:, b, j:j + 1], ALU.subtract, ALU.mult)
                last.then_inc(s_norm, 1)

            def h_lo(g):
                for ib in range(DB):
                    dve.wait_ge(s_hhi, DB * g + ib + 1)
                    hi, lo = (hT[:, a, ib, bass.ds(g * BANK, BANK)] for a in range(2))
                    nc.vector.scalar_tensor_tensor(lo, ps[:, HT_BANK + ib, :], 0.0, hi.bitcast(f32), ALU.max,
                                                   ALU.subtract).then_inc(s_hlo, 1)

            def v_bias(g, free):
                for j in range(2):
                    dve.wait_ge(s_vmm, 2 * g + j + 1)
                    if free:
                        dve.wait_ge(s_vlo, 2 * (g - 1) + j + 1)
                    passed(dve)
                    at = ps[:, V_BANKS[j]:V_BANKS[j] + 2, :]
                    nc.vector.tensor_scalar(row_terms[:, bass.ds(GT * g + 2 * j, 2)], at[:, :, D],
                                            term_bias[:, :], 2 * QSCALE, ALU.add, ALU.mult).then_inc(s_term, 1)
                    nc.vector.tensor_tensor(v_sum[:, j], at[:, :, 0:D], bv_rows[:, :, :], ALU.add)\
                        .then_inc(s_vs, 1)

            def turn_terms(n, groups):
                dve.wait_ge(s_term, 2 * groups)
                nc.vector.transpose(terms_turned[:, n], row_terms[:, :]).then_inc(s_turn, 1)

            def prelude_step(g, b, i_next, b_next, stat=True, free=True, last=False):
                if stat:
                    dve.wait_ge(s_x[b_next], 16 * QN * i_next + 16 * QN)
                    group_stats(g + 1, b_next)
                h_lo(g)
                if stat:
                    normalize(g + 1, b_next)
                if not last:
                    v_bias(g - 1, free)

            dve.wait_ge(s_x[0], 16 * QN)
            group_stats(0, 0)
            for w in range(2):
                dve.wait_ge(s_nhi, w + 1)
                nc.vector.tensor_tensor(wqk[:, w, 1], w_nat[:, w], wqk[:, w, 0].bitcast(f32),
                                        ALU.subtract).then_inc(s_nlo, 1)
            normalize(0, 0)
            dve.wait_ge(s_bias, 16 * 4)
            dve.wait_ge(s_const, 1)
            nc.vector.tensor_tensor(bias_products[:, :], bq_col[:, :], bk_pair[:, :, 0], ALU.mult).then_inc(s_bb, 1)
            dve.wait_ge(s_whi, 1)
            nc.vector.tensor_tensor(wv_T[:, 1, :, 0:D], ps[:, WV_BANK, :].rearrange("p (i o) -> p i o", i=DB),
                                    wv_T[:, 0, :, 0:D].bitcast(f32), ALU.subtract).then_inc(s_wlo, 1)
            dve.wait_ge(s_x[1], 16 * QN)
            group_stats(1, 1)
            h_lo(0)
            normalize(1, 1)
            dve.wait_ge(s_ghi, 1)
            nc.vector.tensor_tensor(G[:, 1], ps[:, G_BANK, :].rearrange("p (i o) -> p i o", i=DB),
                                    G[:, 0].bitcast(f32), ALU.subtract).then_inc(s_glo, 1)
            dve.wait_ge(s_bcol, 1)
            nc.vector.tensor_tensor(wv_T[:, 1, :, D:D + 2],
                                    ps[:, BIAS_BANK, 0:2 * DB].rearrange("p (i n) -> p i n", n=2),
                                    wv_T[:, 0, :, D:D + 2].bitcast(f32), ALU.subtract).then_inc(s_ulo, 1)
            prelude_step(1, 1, 1, 0, free=False)
            with dve.Fori(1, GROUPS // 2 - 1) as i:
                prelude_step(2 * i, 0, i, 1)
                prelude_step(2 * i + 1, 1, i + 1, 0)
            prelude_step(GROUPS - 2, 0, GROUPS // 2 - 1, 1)
            turn_terms(0, GROUPS - 2)
            prelude_step(GROUPS - 1, 1, 0, 0, stat=False, last=True)

            def add_adj(t, i, b, c):
                dve.wait_ge(s_score, CH * t + c + 1)
                if c % CC == 0:
                    dve.wait_ge(s_adj[b][c // CC], 16 * i + 16)
                passed(dve)
                at = logits[:, b, c * BANK:(c + 1) * BANK]
                nc.vector.tensor_tensor_reduce(out=at, in0=ps[:, c % SB, :], in1=at, scale=2.0, scalar=LOWEST,
                                               op0=ALU.add, op1=ALU.max,
                                               accum_out=chunk_max[:, b, c:c + 1]).then_inc(s_logit, 1)

            def row_max(t, i, b, free):
                dve.wait_ge(s_logit, CH * t + CH)
                if free:
                    dve.wait_ge(s_exp, CH * (t - 1))
                nc.vector.tensor_reduce(out=minus_max[:, :], in_=chunk_max[:, b], axis=AX.X, op=ALU.max,
                                        negate=True).then_inc(s_rmax, 1)
                dve.wait_ge(s_tin[b], 16 * i + 16)
                dve.wait_ge(s_rmax, t + 1)
                passed(dve)
                term = row_term[:, b:b + 1]
                nc.vector.scalar_tensor_tensor(neg_max[:, b:b + 1], minus_max[:, :], term, term, ALU.subtract,
                                               ALU.add).then_inc(s_max, 1)

            def transpose_blocks(t, b, c):
                dve.wait_ge(s_exp, CH * t + CC * c + CC)
                at = logits[:, b, c * CLS:(c + 1) * CLS]
                nc.vector.transpose(at, at).then_inc(s_blk, 1)

            def p_lo(t, b, c, place=None):
                dve.wait_ge(s_phi, CH * t + c + 1)
                hi, lo = ((pT[:, c % 2] if place is None else place)[:, a]
                          .rearrange("p (k a q) -> p k a q", k=KB, a=QN) for a in range(2))
                nc.vector.tensor_tensor(lo, landed[b][:, :, c * P:(c + 1) * P]
                                        .rearrange("p a (k q) -> p k a q", k=KB),
                                        hi.bitcast(f32), ALU.subtract).then_inc(s_plo, 1)

            def invert_sum(t, b):
                dve.wait_ge(s_exp, CH * t + CH)
                nc.vector.reduce_sum(row_sum[:, :], chunk_sum[:, b], axis=AX.X).then_inc(s_sum, 1)
                dve.wait_ge(s_sum, t + 1)
                nc.vector.reciprocal(inv_sum[:, b:b + 1], row_sum[:, :]).then_inc(s_inv, 1)

            def finish(t, b):
                dve.wait_ge(s_half, t + 1)
                nc.vector.tensor_tensor(half_out, ps[:, O_BANK + b, 0:D], half_out,
                                        ALU.add).then_inc(s_add, 1)
                dve.wait_ge(s_add, t + 1)
                dve.wait_ge(s_inv, t + 1)
                dve.wait_ge(s_xr, 16 * t + 16)
                nc.vector.scalar_tensor_tensor(x_res, half_out, inv_sum[:, b:b + 1], x_res,
                                               ALU.mult, ALU.add).then_inc(s_fin, 1)

            def period(t, i, b, score=True, soft=True, values=True, fin_at=5):
                for c in range(CH):
                    if values and c < CH - 1:
                        p_lo(t - 2, b, c + 1)
                    if score:
                        add_adj(t, i, b, c)
                        if c == CH - 1:
                            row_max(t, i, b, values)
                    if soft and 1 <= c <= QN:
                        transpose_blocks(t - 1, 1 - b, c - 1)
                    if c == fin_at:
                        finish(t - 3, 1 - b)
                    if values and c == CH - 2:
                        invert_sum(t - 2, b)
                    if soft and c == CH - 1:
                        p_lo(t - 1, 1 - b, 0)

            for c in range(CH):
                add_adj(0, 0, 0, c)
            row_max(0, 0, 0, False)
            transpose_blocks(0, 0, 0)
            v_bias(GROUPS - 2, True)
            transpose_blocks(0, 0, 1)
            v_bias(GROUPS - 1, True)
            transpose_blocks(0, 0, 2)
            transpose_blocks(0, 0, 3)
            turn_terms(1, GROUPS)
            for c in range(CH):
                if c == CH - 1:
                    p_lo(0, 0, 0)
                add_adj(1, 0, 1, c)
            row_max(1, 0, 1, False)
            period(2, 1, 0, fin_at=None)
            period(3, 1, 1)
            with dve.Fori(2, TILES // 2 - 1) as i:
                period(2 * i, i, 0)
                period(2 * i + 1, i, 1)
            t, i = TILES - 1, TILES // 2 - 1
            period(t - 1, i, 0)
            turned_after = (CH // 2, CH - 1, CH + 1, CH + 3)

            def last_p_lo(n):
                u = t - 2 + n // CH
                p_lo(u, u % 2, n % CH, last_place(n))

            last_p_lo(1)
            for c in range(CH):
                if c == CH - 1:
                    last_p_lo(2)
                add_adj(t, i, 1, c)
                if 1 <= c <= QN:
                    transpose_blocks(t - 1, 0, c - 1)
            row_max(t, i, 1, True)
            invert_sum(t - 2, 1)
            finish(t - 3, 0)
            for n in range(3, 3 * CH):
                last_p_lo(n)
                if n in turned_after:
                    transpose_blocks(t, 1, turned_after.index(n))
                if n in (CH + 4, 2 * CH + 2):
                    finish(t - 3 + n // CH, (n // CH) % 2)
                    invert_sum(t - 2 + n // CH, (n // CH + 1) % 2)
            finish(t, 1)


_INS = ["x", "adj", "L0_gnn_Wq", "L0_gnn_bq", "L0_gnn_Wk", "L0_gnn_bk", "L0_gnn_Wv", "L0_gnn_bv"]


def kernel(**inputs):
    import numpy as np
    import concourse.bacc as bacc
    from concourse.bass_utils import run_bass_kernel_spmd

    nc = bacc.Bacc("TRN2", target_bir_lowering=False, num_devices=1)
    arrays, args = {}, []
    for name in _INS:
        a = np.ascontiguousarray(inputs[name])
        arrays[f"in_{name}"] = a
        args.append(nc.dram_tensor(f"in_{name}", a.shape, mybir.dt.from_np(a.dtype), kind="ExternalInput").ap())
    out = nc.dram_tensor("out", inputs["x"].shape, mybir.dt.float32, kind="ExternalOutput").ap()
    graph_attention_kernel(nc, *args, out)
    result = run_bass_kernel_spmd(nc, [arrays], core_ids=[0])
    return result.results[0]["out"]
```
